# Optimizing a Trainium2 kernel written in Bass

```python
import numpy as np
import jax
import jax.numpy as jnp

def _softmax(x, axis=-1):
    return jax.nn.softmax(x, axis=axis)

def _gelu(x):
    return jax.nn.gelu(x, approximate=True)

def _silu(x):
    return jax.nn.silu(x)

def _sigmoid(x):
    return jax.nn.sigmoid(x)

def _layernorm(x, axis=-1, eps=1e-05):
    m = jnp.mean(x, axis=axis, keepdims=True)
    v = jnp.var(x, axis=axis, keepdims=True)
    return (x - m) / jnp.sqrt(v + eps)

def _scatter_add(tgt, idx, src, axis=0):
    return tgt.at[idx].add(src)

def _segment_sum(src, seg, n):
    return jax.ops.segment_sum(src, seg, n)
kernel_name = 'mk_perceiver_d1_seqx_r4_7905e2'

def setup_inputs(seed: int=0):
    np.random.seed(seed)
    _w = jnp.asarray

    def _rec_inputs():
        import jax
        import jax.numpy as jnp
        _rk = jax.random.key(seed)
        x = -0.0002928 + 1 * jax.random.normal(jax.random.fold_in(_rk, 1), (2, 256, 256), jnp.float32)
        _lenS = 256 - jax.random.randint(jax.random.fold_in(_rk, 7), (2,), 0, max(1, 256 // 4) + 1, jnp.int32)
        _lenS2 = 4096 - jax.random.randint(jax.random.fold_in(_rk, 8), (2,), 0, max(1, 4096 // 4) + 1, jnp.int32)
        _ctx_1024P = jax.random.normal(jax.random.fold_in(_rk, 11), (2, 16, 256), jnp.float32)
        _ctx_1024c = jax.random.dirichlet(jax.random.fold_in(_rk, 511), 0.3 * jnp.ones((16,), jnp.float32), (2, 4096))
        _ctx_1024t = jnp.einsum('bsk,bkd->bsd', _ctx_1024c, _ctx_1024P)
        _ctx_1024t = _ctx_1024t * jax.lax.rsqrt(jnp.mean(jnp.square(_ctx_1024t)) + 1e-12) * 0.953939
        ctx_1024 = -1.39393e-06 + 0.999914 * (_ctx_1024t + 0.3 * jax.random.normal(jax.random.fold_in(_rk, 611), (2, 4096, 256), jnp.float32))
        return (x, ctx_1024)
    x, ctx_1024 = _rec_inputs()

    def _L0_xattn_setup():
        import jax, jax.numpy as jnp
        import numpy as np
        DIM = 256
        NUM_HEADS = 16
        HEAD_DIM = DIM // NUM_HEADS
        key = jax.random.key(seed)
        ks = jax.random.split(key, 11)
        B, N, C = (2, 512, DIM)
        s = 1.0 / np.sqrt(C)
        inp = {'q': jax.random.normal(ks[0], (B, N, C), jnp.float32), 'k': jax.random.normal(ks[1], (B, N, C), jnp.float32), 'v': jax.random.normal(ks[2], (B, N, C), jnp.float32), 'Wq': jax.random.normal(ks[3], (C, C), jnp.float32) * s, 'bq': jnp.zeros((C,), jnp.float32), 'Wk': jax.random.normal(ks[4], (C, C), jnp.float32) * s, 'bk': jnp.zeros((C,), jnp.float32), 'Wv': jax.random.normal(ks[5], (C, C), jnp.float32) * s, 'bv': jnp.zeros((C,), jnp.float32), 'Wo': jax.random.normal(ks[6], (C, C), jnp.float32) * s, 'bo': jnp.zeros((C,), jnp.float32)}
        return inp
    _L0_xattn_all = _L0_xattn_setup()
    _L0_xattn_in = {k: v for k, v in _L0_xattn_all.items() if k in ('Wq', 'bq', 'Wk', 'bk', 'Wv', 'bv', 'Wo', 'bo')}
    del _L0_xattn_all

    def _L0_attn_setup():
        import jax, jax.numpy as jnp
        import numpy as np
        N_EMBD = 256
        N_HEAD = 16
        HEAD_DIM = N_EMBD // N_HEAD
        KV_RANK = 64
        Q_RANK = 128
        ROPE_DIM = 32
        B, T = (2, 512)
        EPS = 1e-06

        def _rope_tables(T, dim):
            inv_freq = 1.0 / 10000.0 ** (np.arange(0, dim, 2, dtype=np.float32) / dim)
            t = np.arange(T, dtype=np.float32)
            freqs = np.outer(t, inv_freq)
            emb = np.concatenate([freqs, freqs], -1)
            return (jnp.asarray(np.cos(emb)), jnp.asarray(np.sin(emb)))

        def _apply_rope(x, cos, sin):
            d2 = x.shape[-1] // 2
            x1, x2 = (x[..., :d2], x[..., d2:])
            rot = jnp.concatenate([-x2, x1], axis=-1)
            return x * cos[None, None, :, :] + rot * sin[None, None, :, :]
        key = jax.random.key(seed)
        ks = jax.random.split(key, 10)

        def w(k, fan_in, fan_out):
            return jax.random.normal(k, (fan_in, fan_out), dtype=jnp.float32) * fan_in ** (-0.5)
        return {'x': jax.random.normal(ks[0], (B, T, N_EMBD), dtype=jnp.float32), 'W_kv': w(ks[1], N_EMBD, KV_RANK), 'g_kv': jnp.ones((KV_RANK,), dtype=jnp.float32), 'W_kdec': w(ks[2], KV_RANK, N_HEAD * HEAD_DIM), 'W_vdec': w(ks[3], KV_RANK, N_HEAD * HEAD_DIM), 'W_q': w(ks[4], N_EMBD, Q_RANK), 'W_qdec': w(ks[5], Q_RANK, N_HEAD * HEAD_DIM), 'W_krope': w(ks[6], N_EMBD, N_HEAD * ROPE_DIM), 'W_qrope': w(ks[7], Q_RANK, N_HEAD * ROPE_DIM), 'W_o': w(ks[8], N_HEAD * HEAD_DIM, N_EMBD)}
    _L0_attn_all = _L0_attn_setup()
    _L0_attn_in = {k: v for k, v in _L0_attn_all.items() if k in ('W_kv', 'g_kv', 'W_kdec', 'W_vdec', 'W_q', 'W_qdec', 'W_krope', 'W_qrope', 'W_o')}
    del _L0_attn_all

    def _L0_ffn_setup():
        import jax, jax.numpy as jnp
        import numpy as np
        D_MODEL = 256
        D_FF = 1024
        N_EXPERTS = 8
        INIT_SCALE = 0.1

        def _trunc_normal(key, shape, std):
            return std * jax.random.truncated_normal(key, -2.0, 2.0, shape, dtype=jnp.float32)
        key = jax.random.key(seed)
        ks = jax.random.split(key, 5)
        x = jax.random.normal(ks[0], (4, 256, D_MODEL), dtype=jnp.float32)
        router_W = _trunc_normal(ks[1], (D_MODEL, N_EXPERTS), INIT_SCALE / np.sqrt(D_MODEL))
        router_b = jnp.zeros((N_EXPERTS,), dtype=jnp.float32)
        W1 = _trunc_normal(ks[2], (N_EXPERTS, D_MODEL, D_FF), INIT_SCALE / np.sqrt(D_MODEL))
        b1 = jnp.zeros((N_EXPERTS, D_FF), dtype=jnp.float32)
        W2 = _trunc_normal(ks[3], (N_EXPERTS, D_FF, D_MODEL), INIT_SCALE / np.sqrt(D_FF))
        b2 = jnp.zeros((N_EXPERTS, D_MODEL), dtype=jnp.float32)
        return {'x': x, 'router_W': router_W, 'router_b': router_b, 'W1': W1, 'b1': b1, 'W2': W2, 'b2': b2}
    _L0_ffn_all = _L0_ffn_setup()
    _L0_ffn_in = {k: v for k, v in _L0_ffn_all.items() if k in ('router_W', 'router_b', 'W1', 'b1', 'W2', 'b2')}
    del _L0_ffn_all
    return {'x': x, 'ctx_1024': ctx_1024, 'L0_xattn_Wq': _L0_xattn_in['Wq'], 'L0_xattn_bq': _L0_xattn_in['bq'], 'L0_xattn_Wk': _L0_xattn_in['Wk'], 'L0_xattn_bk': _L0_xattn_in['bk'], 'L0_xattn_Wv': _L0_xattn_in['Wv'], 'L0_xattn_bv': _L0_xattn_in['bv'], 'L0_xattn_Wo': _L0_xattn_in['Wo'], 'L0_xattn_bo': _L0_xattn_in['bo'], 'L0_attn_W_kv': _L0_attn_in['W_kv'], 'L0_attn_g_kv': _L0_attn_in['g_kv'], 'L0_attn_W_kdec': _L0_attn_in['W_kdec'], 'L0_attn_W_vdec': _L0_attn_in['W_vdec'], 'L0_attn_W_q': _L0_attn_in['W_q'], 'L0_attn_W_qdec': _L0_attn_in['W_qdec'], 'L0_attn_W_krope': _L0_attn_in['W_krope'], 'L0_attn_W_qrope': _L0_attn_in['W_qrope'], 'L0_attn_W_o': _L0_attn_in['W_o'], 'L0_ffn_router_W': _L0_ffn_in['router_W'], 'L0_ffn_router_b': _L0_ffn_in['router_b'], 'L0_ffn_W1': _L0_ffn_in['W1'], 'L0_ffn_b1': _L0_ffn_in['b1'], 'L0_ffn_W2': _L0_ffn_in['W2'], 'L0_ffn_b2': _L0_ffn_in['b2']}

def reference(x, ctx_1024, L0_xattn_Wq, L0_xattn_bq, L0_xattn_Wk, L0_xattn_bk, L0_xattn_Wv, L0_xattn_bv, L0_xattn_Wo, L0_xattn_bo, L0_attn_W_kv, L0_attn_g_kv, L0_attn_W_kdec, L0_attn_W_vdec, L0_attn_W_q, L0_attn_W_qdec, L0_attn_W_krope, L0_attn_W_qrope, L0_attn_W_o, L0_ffn_router_W, L0_ffn_router_b, L0_ffn_W1, L0_ffn_b1, L0_ffn_W2, L0_ffn_b2):
    import jax
    import jax.numpy as jnp

    def _L0_xattn_ref(q, k, v, Wq, bq, Wk, bk, Wv, bv, Wo, bo):
        import jax, jax.numpy as jnp
        import numpy as np
        DIM = 256
        NUM_HEADS = 16
        HEAD_DIM = DIM // NUM_HEADS
        B, Nq, C = q.shape
        Nkv = k.shape[1]
        H, D = (NUM_HEADS, HEAD_DIM)
        qh = (q @ Wq.T + bq).reshape(B, Nq, H, D).transpose(0, 2, 1, 3)
        kh = (k @ Wk.T + bk).reshape(B, Nkv, H, D).transpose(0, 2, 1, 3)
        vh = (v @ Wv.T + bv).reshape(B, Nkv, H, D).transpose(0, 2, 1, 3)
        scale = D ** (-0.5)
        attn = jax.nn.softmax(jnp.einsum('bhqd,bhkd->bhqk', qh, kh) * scale, axis=-1)
        out = jnp.einsum('bhqk,bhkd->bhqd', attn, vh)
        out = out.transpose(0, 2, 1, 3).reshape(B, Nq, C)
        return out @ Wo.T + bo

    def _L0_attn_ref(x, W_kv, g_kv, W_kdec, W_vdec, W_q, W_qdec, W_krope, W_qrope, W_o):
        import jax, jax.numpy as jnp
        import numpy as np
        N_EMBD = 256
        N_HEAD = 16
        HEAD_DIM = N_EMBD // N_HEAD
        KV_RANK = 64
        Q_RANK = 128
        ROPE_DIM = 32
        B, T = (2, 512)
        EPS = 1e-06

        def _rope_tables(T, dim):
            inv_freq = 1.0 / 10000.0 ** (np.arange(0, dim, 2, dtype=np.float32) / dim)
            t = np.arange(T, dtype=np.float32)
            freqs = np.outer(t, inv_freq)
            emb = np.concatenate([freqs, freqs], -1)
            return (jnp.asarray(np.cos(emb)), jnp.asarray(np.sin(emb)))

        def _apply_rope(x, cos, sin):
            d2 = x.shape[-1] // 2
            x1, x2 = (x[..., :d2], x[..., d2:])
            rot = jnp.concatenate([-x2, x1], axis=-1)
            return x * cos[None, None, :, :] + rot * sin[None, None, :, :]
        Bx, Tx, C = x.shape
        kv_c = x @ W_kv
        kv_c = kv_c * jax.lax.rsqrt(jnp.mean(kv_c * kv_c, axis=-1, keepdims=True) + EPS) * g_kv
        q_c = x @ W_q

        def heads(y, d):
            return y.reshape(Bx, Tx, N_HEAD, d).transpose(0, 2, 1, 3)
        k_content = heads(kv_c @ W_kdec, HEAD_DIM)
        v = heads(kv_c @ W_vdec, HEAD_DIM)
        q_content = heads(q_c @ W_qdec, HEAD_DIM)
        k_rope = heads(x @ W_krope, ROPE_DIM)
        q_rope = heads(q_c @ W_qrope, ROPE_DIM)
        cos, sin = _rope_tables(Tx, ROPE_DIM)
        q_rope = _apply_rope(q_rope, cos, sin)
        k_rope = _apply_rope(k_rope, cos, sin)
        q = jnp.concatenate([q_content, q_rope], axis=-1)
        k = jnp.concatenate([k_content, k_rope], axis=-1)
        scale = 1.0 / jnp.sqrt(jnp.float32(q.shape[-1]))
        scores = jnp.einsum('bhqd,bhkd->bhqk', q, k) * scale
        causal = jnp.tril(jnp.ones((Tx, Tx), dtype=bool))
        scores = jnp.where(causal[None, None], scores, jnp.float32(-jnp.inf))
        attn = jax.nn.softmax(scores, axis=-1)
        out = jnp.einsum('bhqk,bhkd->bhqd', attn, v)
        out = out.transpose(0, 2, 1, 3).reshape(Bx, Tx, N_HEAD * HEAD_DIM)
        return out @ W_o

    def _L0_ffn_ref(x, router_W, router_b, W1, b1, W2, b2):
        import jax, jax.numpy as jnp
        import numpy as np
        D_MODEL = 256
        D_FF = 1024
        N_EXPERTS = 8
        INIT_SCALE = 0.1

        def _trunc_normal(key, shape, std):
            return std * jax.random.truncated_normal(key, -2.0, 2.0, shape, dtype=jnp.float32)
        logits = jnp.einsum('bsd,de->bse', x.astype(jnp.float32), router_W) + router_b
        probs = jax.nn.softmax(logits, axis=-1)
        top1 = jnp.argmax(probs, axis=-1)
        mask = jax.nn.one_hot(top1, N_EXPERTS, dtype=x.dtype)
        gates = mask * probs.astype(x.dtype)
        h = jax.nn.relu(jnp.einsum('bsd,edf->besf', x, W1) + b1[:, None, :])
        y = jnp.einsum('besf,efd->besd', h, W2) + b2[:, None, :]
        out = jnp.einsum('bse,besd->bsd', gates, y)
        return out
    x = x + _L0_xattn_ref(_layernorm(x, axis=-1), ctx_1024, ctx_1024, L0_xattn_Wq, L0_xattn_bq, L0_xattn_Wk, L0_xattn_bk, L0_xattn_Wv, L0_xattn_bv, L0_xattn_Wo, L0_xattn_bo)
    x = x + _L0_attn_ref(_layernorm(x, axis=-1), L0_attn_W_kv, L0_attn_g_kv, L0_attn_W_kdec, L0_attn_W_vdec, L0_attn_W_q, L0_attn_W_qdec, L0_attn_W_krope, L0_attn_W_qrope, L0_attn_W_o)
    x = x + _L0_ffn_ref(_layernorm(x, axis=-1), L0_ffn_router_W, L0_ffn_router_b, L0_ffn_W1, L0_ffn_b1, L0_ffn_W2, L0_ffn_b2)
    return x

_drawn_inputs = setup_inputs


def setup_inputs(seed=0):
    import zlib

    import numpy as np

    out = dict(_drawn_inputs(seed))
    spreads = {'L0_xattn_bq': (0.0, 0.353),
     'L0_xattn_bk': (0.0, 0.8),
     'L0_xattn_bv': (0.0, 0.1),
     'L0_xattn_bo': (0.0, 0.1),
     'L0_attn_g_kv': (1.0, 0.2),
     'L0_ffn_router_b': (0.0, 0.623),
     'L0_ffn_b1': (0.0, 0.8),
     'L0_ffn_b2': (0.0, 0.678)}
    factors = {'L0_ffn_router_W': 5.903, 'L0_ffn_W1': 8.0, 'L0_ffn_W2': 8.0}
    for name, (base, spread) in spreads.items():
        noise = np.random.default_rng([zlib.crc32(name.encode()), seed]).standard_normal(out[name].shape)
        drawn = base * np.exp(spread * noise) if base else spread * noise
        out[name] = jnp.asarray(drawn.astype(out[name].dtype))
    for name, factor in factors.items():
        out[name] = (out[name] * factor).astype(out[name].dtype)
    return out
```

```python
from contextlib import ExitStack

import numpy as np

import concourse.bass as bass
from concourse import mybir

F32 = mybir.dt.float32
BF16 = mybir.dt.bfloat16
ALU = mybir.AluOpType
ACT = mybir.ActivationFunctionType
AXX = mybir.AxisListType.X

P = 128
B, NQ, C = 2, 256, 256
NKV = 4096
H, D = 16, 16
TOK = B * NQ
TT = TOK // P
KT = C // P
CHUNK = 512
NCHUNK = B * NKV // CHUNK
CT = CHUNK // P
HG = 4
GROUPS = H // HG
NG = B * GROUPS
UNITS = NKV // P
QUARTERS = 4
MAXC = NKV // CHUNK
STACK = 6 * D
LN_EPS = 1e-5
E = 8
F = 1024
FT = F // P
TILES = TOK // P + E - 1


def wait_past(eng, sem, value):
    if not (isinstance(value, int) and value <= 0):
        eng.wait_ge(sem, value)


class Steps:

    def __init__(self, eng, sem):
        self.eng, self.sem, self.n, self.shift = eng, sem, 0, 0

    def mark(self, ins):
        self.n += 1
        ins.then_inc(self.sem, 1)
        return self.n + self.shift

    def link(self, ins):
        self.eng.wait_ge(self.sem, self.mark(ins))


def cross_attention(nc, top, t):
    with ExitStack() as ctx:
        def sb(name, shape, dt=F32):
            return ctx.enter_context(nc.sbuf_tensor(name, shape, dt))

        def ps(name, shape):
            return ctx.enter_context(nc.psum_tensor(name, shape, F32))

        def sem(name):
            return ctx.enter_context(nc.semaphore(name))

        x1, ident, identb = t["x1"], t["ident"], t["identb"]

        k_parts = nc.dram_tensor("k_parts", [NG, 3 * D, HG, NKV], BF16).ap()
        q_stack = nc.dram_tensor("q_stack", [NG, STACK, HG, NQ], BF16).ap()
        Q_ROWS = (0, 0, 0, 1, 1, 2)
        v_rows = nc.dram_tensor("v_rows", [NG, P, UNITS, HG, D + 1], F32).ap()

        wq = sb("wq", [P, KT, C])
        wk = sb("wk", [P, KT, C])
        wv = sb("wv", [P, KT, C])
        wo = sb("wo", [P, KT, C])
        bq = sb("bq", [P, KT])
        bk = sb("bk", [P, KT])
        bv = sb("bv", [P, KT])
        bo = sb("bo", [P, C])
        x = sb("x", [P, TT, C])
        xn = sb("xn", [P, TT, C])
        xT = sb("xT", [P, KT, TOK])
        stats = sb("stats", [P, TT, 6])
        mv = sb("mv", [P, TT, 2])
        sd = sb("sd", [P, TT, 2])
        ctx_in = [sb(f"ctx_in{i}", [P, CT, C]) for i in range(2)]
        ctxT = [sb(f"ctxT{i}", [P, KT, CHUNK]) for i in range(2)]
        kf = sb("kf", [P, KT, CHUNK])
        rest = sb("rest", [P, KT, CHUNK])
        parts = [sb(f"parts{i}", [P, KT, 3, CHUNK], BF16) for i in range(2)]
        q3 = sb("q3", [P, KT, 3, TOK], BF16)
        v_out = [sb(f"v_out{i}", [P, GROUPS, CT, HG, D + 1]) for i in range(2)]
        kst = [sb(f"kst{i}", [STACK + 2, HG, NKV], BF16) for i in range(2)]
        qst = [sb(f"qst{i}", [STACK + 2, HG, NQ], BF16) for i in range(2)]
        vg = [sb(f"vg{i}", [P, UNITS, HG, D + 1]) for i in range(2)]
        probs = [sb(f"probs{i}", [P, HG, NQ]) for i in range(4)]
        maxes = sb("maxes", [P, HG * 2, MAXC])
        mrow = sb("mrow", [P, HG * 2])
        shift = sb("shift", [P, HG * 2, 2], BF16)
        acc_s = sb("acc_s", [P, NQ])
        recip = sb("recip", [P, 2, HG])
        o = sb("o", [P, 2, NG, HG, D])
        oT = sb("oT", [P, KT, TOK])

        banks = [ps(f"bank{i}", [P, 512]) for i in range(4)]
        score_a = ps("score_a", [P, HG, NQ])
        score_b = ps("score_b", [P, HG, NQ])

        side = [bank[:, :] for bank in banks[0:3]]
        acc = banks[3][:, 0:NQ]
        scores = [score_a[:, :, :].rearrange("p h n -> p (h n)"), score_b[:, :, :].rearrange("p h n -> p (h n)")]

        s_w = sem("weights_in")
        s_ctx = [sem(f"ctx_in_{i}") for i in range(2)]
        s_id = sem("ident_ready")
        s_ones = sem("ones_ready")
        s_v = sem("vector_steps")
        s_var = sem("variance_ready")
        s_qf = sem("query_product_copied")
        s_sd = sem("deviation_ready")
        s_xn = sem("normed_ready")
        s_xt = sem("x_transposed")
        s_xts = sem("x_transposed_copied")
        s_qp = sem("query_product")
        s_qs = sem("query_parts_ready")
        s_qst = sem("query_parts_stored")
        s_tp = sem("ctx_transposed")
        s_tc = sem("ctx_transposed_copied")
        s_kp = sem("key_product")
        s_kf = sem("keys_copied")
        s_kh = sem("key_high_ready")
        s_kr = sem("key_parts_ready")
        s_vp = sem("value_product")
        s_vr = sem("values_ready")
        s_ks = [sem(f"key_parts_stored_{i}") for i in range(2)]
        s_vs = [sem(f"values_stored_{i}") for i in range(2)]
        s_kq = [[sem(f"key_stack_in_{i}_{q}") for q in range(QUARTERS)] for i in range(2)]
        s_q = [sem(f"query_stack_in_{i}") for i in range(2)]
        s_vg = [sem(f"group_values_in_{i}") for i in range(2)]
        s_sc = sem("scores_ready")
        s_ex = sem("probs_ready")
        s_pf = sem("probs_free")
        s_af = sem("acc_free")
        s_job = sem("side_bank_written")
        s_jd = sem("side_bank_read")
        s_sh = sem("shift_ready")
        s_ot = sem("out_transposed")
        s_otc = sem("out_transposed_copied")
        s_y = sem("out_product")

        LOADS = 9

        HEAD_PAIR = 5
        head_banks = [score_b[:, 0:2, :].rearrange("p a n -> p (a n)"), score_b[:, 2:4, :].rearrange("p a n -> p (a n)")]

        def head_range(n):
            chunks, jobs = NCHUNK - 2 * HEAD_PAIR, HG * 2 * MAXC
            a = n - 2 * HEAD_PAIR
            return jobs * a // chunks, jobs * (a + 1) // chunks

        def free_job(p, base):
            return base + (p - 2 if p >= 3 else {0: -1, 1: 0, 2: -2}[p])

        HEAD_JOBS = HG * 2 * MAXC + 2
        BODY_JOBS = HEAD_JOBS + 1
        FIRST_T, LAST_T = 2, 27

        def max_jobs_at(tile):
            n, span = HG * 2 * MAXC, LAST_T - FIRST_T + 1
            a = n * max(0, min(span, tile - FIRST_T)) // span
            b = n * max(0, min(span, tile - FIRST_T + 1)) // span
            return range(a, b)

        block = ctx.enter_context(nc.Block())

        @block.gpsimd
        def _(eng):
            eng.memset(ident[:, :], 0.0).then_inc(s_pf, len(probs))
            eng.memset(identb[:, :], 0.0).then_inc(s_id, 1)
            eng.wait_ge(s_pf, len(probs))
            eng.wait_ge(s_id, 1)
            for m in (ident, identb):
                eng.affine_select(out=m[:, :], in_=m[:, :], compare_op=ALU.not_equal, fill=1.0,
                                  base=0, pattern=[[-1, P]], channel_multiplier=1).then_inc(s_id, 1)
            eng.wait_ge(s_id, 3)
            for n, v in enumerate(v_out):
                eng.memset(v[:], 1.0).then_inc(s_ones, 1)
                eng.wait_ge(s_ones, n + 1)
            for n, k in enumerate(kst):
                eng.memset(k[STACK:STACK + 2, :, :], 1.0).then_inc(s_ones, 1)
                eng.wait_ge(s_ones, n + 3)

        @block.sync
        def _(sp):
            sp.dma_start(x[:], t["x_in"].rearrange("b (q p) c -> p (b q) c", p=P)).then_inc(s_w, 16)
            for dst, src in ((wq, t["wq"]), (wk, t["wk"]), (wv, t["wv"]), (wo, t["wo"])):
                sp.dma_start(dst[:], src.rearrange("(k p) n -> p k n", p=P)).then_inc(s_w, 16)
            for dst, src in ((bq, t["bq"]), (bk, t["bk"]), (bv, t["bv"])):
                sp.dma_start(dst[:], src).then_inc(s_w, 16)
            sp.dma_start(bo[:], t["bo"].partition_broadcast(P)).then_inc(s_w, 16)

            ctx_rows = t["ctx"].rearrange("b (n p j) c -> p (b n) j c", p=P, j=CT)
            for s in range(2):
                sp.dma_start(ctx_in[s][:], ctx_rows[:, s, :, :]).then_inc(s_ctx[s], 16)
            for n, src in t["attn_src"].items():
                sp.dma_start(t["attn_w"][n][:], src).then_inc(t["s_aw"], 16)
            sp.wait_ge(s_qs, 1)
            R = HG * D
            for copy, part in enumerate(Q_ROWS):
                for g in range(2):
                    for b in range(B):
                        i = b * GROUPS + g * KT
                        dst = q_stack[i:i + KT, copy * D:(copy + 1) * D, :, :]
                        sp.dma_start(dst.rearrange("k d j n -> (d j) k n"),
                                     q3[g * R:(g + 1) * R, :, part, b * NQ:(b + 1) * NQ]).then_inc(s_qst, 16)

            HALF = NKV // CHUNK

            def store(s, n, b, cn):
                sp.wait_ge(s_kr, n + 1)
                for g in range(2):
                    i = b * GROUPS + g * KT
                    dst = k_parts[i:i + KT, :, :, bass.ds(cn * CHUNK, CHUNK)]
                    sp.dma_start(dst.rearrange("k (a d) j n -> (d j) (k a) n", d=D),
                                 parts[s][g * R:(g + 1) * R, :, :, :].rearrange("p k a n -> p (k a) n")).then_inc(s_ks[s], 16)
                sp.wait_ge(s_vr, n + 1)
                dst = v_rows[b * GROUPS:(b + 1) * GROUPS, :, bass.ds(cn * CT, CT), :, :]
                sp.dma_start(dst.rearrange("g p j h e -> p g (j h e)"),
                             v_out[s][:].rearrange("p g j h e -> p g (j h e)")).then_inc(s_vs[s], 16)

            def project(it, b, more):
                for s in range(2):
                    cn = it * 2 + s
                    n = cn + b * HALF
                    if more:
                        sp.wait_ge(s_tp, n + 1)
                        sp.dma_start(ctx_in[s][:], ctx_rows[:, bass.ds(n + 2, 1), :, :].rearrange("p o j c -> p (o j) c")).then_inc(s_ctx[s], 16)
                    store(s, n, b, cn)

            def load_queries(s, i):
                sp.dma_start(qst[s][0:STACK, :, :].rearrange("p j n -> p (j n)"),
                             q_stack[bass.ds(i, 1), :, :, :].rearrange("o p j n -> p (o j n)")).then_inc(s_q[s], 16)

            def load_keys(s, i, q):
                n = NKV // QUARTERS
                row = 0
                for part_rows in (3 * D, 2 * D, D):
                    src = k_parts[bass.ds(i, 1), 0:part_rows, :, q * n:(q + 1) * n].rearrange("o p j n -> p (o j) n")
                    sp.dma_start(kst[s][row:row + part_rows, :, q * n:(q + 1) * n], src).then_inc(s_kq[s][q], 16)
                    row += part_rows

            def load_values(s, i):
                src = v_rows[bass.ds(i, 1), :, :, :, :].rearrange("o p u h e -> p (o u h e)")
                sp.dma_start(vg[s][:].rearrange("p u h e -> p (u h e)"), src).then_inc(s_vg[s], 16)

            with sp.Fori(0, HALF // 2) as it:
                project(it, 0, True)
            sp.wait_ge(s_qst, 16 * 2 * B * len(Q_ROWS))
            for s in range(2):
                sp.wait_ge(s_ks[s], 2 * 16 * (NCHUNK // 4))
                sp.wait_ge(s_vs[s], 16 * (NCHUNK // 4))
            load_queries(0, 0)
            for q in range(QUARTERS):
                load_keys(0, 0, q)
            project(0, 1, True)
            load_queries(1, 1)
            for q in range(QUARTERS):
                load_keys(1, 1, q)
            for i in range(2):
                load_values(i, i)
            with sp.Fori(1, HALF // 2 - 1) as it:
                project(it, 1, True)
            project(HALF // 2 - 1, 1, False)
            for s in range(2):
                sp.wait_ge(s_ks[s], 2 * 16 * (NCHUNK // 2))
                sp.wait_ge(s_vs[s], 16 * (NCHUNK // 2))

            def next_group(s, i):
                for q in range(QUARTERS):
                    if q == QUARTERS - 1:
                        sp.wait_ge(s_sc, (i - 1) * UNITS)
                        load_queries(s, i)
                    sp.wait_ge(s_pf, (i - 2) * UNITS + (len(probs) + (UNITS // QUARTERS) * (q + 1)))
                    load_keys(s, i, q)
                load_values(s, i)

            with sp.Fori(1, NG // 2) as it:
                for s in range(2):
                    next_group(s, it * 2 + s)
            sp.wait_ge(t["s_aw"], 16 * len(t["attn_src"]))

        @block.scalar
        def _(act):
            act.wait_ge(s_var, 1)
            act.activation(sd[:, :, 1], sd[:, :, 0], ACT.Sqrt).then_inc(s_sd, 1)

            def copy_transposed(n, s):
                act.wait_ge(s_tp, n + 1)
                act.activation(ctxT[s][:, 0, :], banks[0][:, :], ACT.Copy).then_inc(s_tc, 1)

            def project(it, more):
                for s in range(2):
                    n = it * 2 + s
                    if more or s == 0:
                        copy_transposed(n + 1, 1 - s)
                    wait_past(act, s_kr, n)
                    for k in range(KT):
                        act.wait_ge(s_kp, n * KT + (k + 1))
                        act.activation(kf[:, k, :], banks[2 + k][:, :], ACT.Identity, bias=bk[:, k:k + 1]).then_inc(s_kf, 1)
                    act.wait_ge(s_kf, n * KT + KT)
                    wait_past(act, s_ks[s], it * 32)
                    act.activation(parts[s][:, :, 0, :], kf[:, :, :], ACT.Copy).then_inc(s_kh, 1)
                    act.wait_ge(s_vp, n + 1)
                    wait_past(act, s_vs[s], it * 16)
                    for g in range(GROUPS):
                        ins = act.activation(v_out[s][:, g, :, :, 0:D],
                                             score_a[:, :, g * HG * D:(g + 1) * HG * D].rearrange("p t (j d) -> p t j d", d=D),
                                             ACT.Copy)
                    ins.then_inc(s_vr, 1)

            act.wait_ge(s_w, LOADS * 16)
            act.wait_ge(s_ones, 4)
            copy_transposed(0, 0)
            project(0, True)
            with act.Fori(1, NCHUNK // 2 - 1) as it:
                project(it, True)
            project(NCHUNK // 2 - 1, False)

            def copy_output(i):
                act.wait_ge(s_pf, (i + 1) * UNITS + len(probs))
                act.activation(acc_s[:], acc, ACT.Copy).then_inc(s_af, 1)

            def probabilities(i, first):
                for u in range(UNITS):
                    n = i * UNITS + u
                    r = u % len(probs)
                    act.wait_ge(s_sc, n + 1)
                    act.wait_ge(s_pf, n + 1)
                    act.activation(probs[r][:].rearrange("p h n -> p (h n)"),
                                   scores[u % 2], ACT.Exp).then_inc(s_ex, 1)
                    if u == 0 and not first:
                        copy_output(i - 1)

            probabilities(0, True)
            with act.Fori(0, (NG - 2) // 2) as it:
                probabilities(it * 2 + 1, False)
                probabilities(it * 2 + 2, False)
            probabilities(NG - 1, False)
            copy_output(NG - 1)

        @block.vector
        def _(dve):
            st = Steps(dve, s_v)
            v = nc.vector
            dve.wait_ge(s_w, LOADS * 16)
            for i in range(TT):
                v.bn_stats(stats[:, i, :], x[:, i, :]).then_inc(s_v, 1)
            st.n = TT
            dve.wait_ge(s_v, TT)
            for i in range(TT):
                last = st.mark(v.bn_aggr(mv[:, i, :], stats[:, i, :]))
            dve.wait_ge(s_v, last)
            v.tensor_scalar(sd[:, :, 0], mv[:, :, 1], LN_EPS, None, ALU.add).then_inc(s_var, 1)
            for i in range(TT):
                v.tensor_tensor(x1[:, i, :], x[:, i, :], bo[:, :], ALU.add)
            dve.wait_ge(s_sd, 1)
            st.link(v.reciprocal(sd[:, :, 0], sd[:, :, 1]))
            for i in range(TT):
                v.tensor_scalar(xn[:, i, :], x[:, i, :], mv[:, i, 0:1], sd[:, i, 0:1],
                                ALU.subtract, ALU.mult).then_inc(s_xn, 1)
            dve.wait_ge(s_xt, 1)
            for k in range(KT):
                v.tensor_copy(xT[:, k, :], banks[k][:, :]).then_inc(s_xts, 1)

            def split(src, dst, mid_sem, high):
                if high:
                    st.link(v.tensor_copy(dst[:, :, 0, :], src))
                st.link(v.tensor_tensor(rest[:], src, dst[:, :, 0, :], ALU.subtract))
                st.link(v.tensor_copy(dst[:, :, 1, :], rest[:]))
                v.tensor_tensor(dst[:, :, 2, :], rest[:], dst[:, :, 1, :], ALU.subtract).then_inc(mid_sem, 1)

            qf = xn[:].rearrange("p a c -> p (a c)").rearrange("p (k n) -> p k n", k=KT)
            dve.wait_ge(s_qp, 1)
            for k in range(KT):
                v.tensor_scalar(qf[:, k, :], banks[2 + k][:, :], bq[:, k:k + 1], D ** -0.5,
                                ALU.add, ALU.mult).then_inc(s_qf, 1)
            dve.wait_ge(s_qf, KT)
            split(qf, q3, s_qs, True)

            def copy_transposed(n, s):
                dve.wait_ge(s_tp, n + 1)
                v.tensor_copy(ctxT[s][:, 1, :], banks[1][:, :]).then_inc(s_tc, 1)

            def max_job(job, slot, k, c):
                dve.wait_ge(s_job, job + 1)
                v.reduce_max(maxes[:, k, c:c + 1], slot[:, :], AXX).then_inc(s_jd, 1)

            def make_shift(job):
                dve.wait_ge(s_jd, job)
                st.link(v.reduce_max(mrow[:], maxes[:], AXX))
                st.link(v.tensor_scalar(shift[:, :, 0], mrow[:], -1.0, None, ALU.mult))
                v.scalar_tensor_tensor(out=shift[:, :, 1], in0=mrow[:], scalar=-1.0, in1=shift[:, :, 0],
                                       op0=ALU.mult, op1=ALU.subtract).then_inc(s_sh, 1)

            def shift_job(job, slot, s, a):
                dve.wait_ge(s_job, job + 1)
                v.tensor_copy(qst[s][STACK:STACK + 2, 2 * a:2 * a + 2, :].rearrange("p h n -> p (h n)"),
                              slot[STACK:STACK + 2, :]).then_inc(s_jd, 1)

            def out_job(job, slot, i):
                dve.wait_ge(s_job, job + 1)
                dve.wait_ge(s_jd, job)
                rows = slot[:, 0:2 * P].rearrange("p (q j r) -> p q j r", q=2, j=HG)
                st.link(v.reciprocal(recip[:], rows[:, :, :, D]))
                v.tensor_tensor(o[:, :, bass.ds(i, 1), :, :].rearrange("p q o j d -> p q (o j) d"),
                                rows[:, :, :, 0:D], recip[:].unsqueeze(3).to_broadcast([P, 2, HG, D]),
                                ALU.mult).then_inc(s_jd, 1)

            PER_PAIR = 4

            def project(it, more, head=None):
                for s in range(2):
                    n = it * 2 + s
                    if more or s == 0:
                        copy_transposed(n + 1, 1 - s)
                    if head:
                        head(n, 0)
                    dve.wait_ge(s_kh, n + 1)
                    wait_past(dve, s_ks[s], it * 32)
                    st.link(v.tensor_tensor(rest[:], kf[:], parts[s][:, :, 0, :], ALU.subtract))
                    if head:
                        head(n, 1)
                    st.link(v.tensor_copy(parts[s][:, :, 1, :], rest[:]))
                    if head:
                        head(n, 2)
                    v.tensor_tensor(parts[s][:, :, 2, :], rest[:], parts[s][:, :, 1, :], ALU.subtract).then_inc(s_kr, 1)
                    if head:
                        head(n, 3)

            def head_jobs(n, step):
                a, b = head_range(n)
                lots = [a, min(a + 5, b), min(a + 7, b), min(a + 9, b), b]
                for m in range(lots[step], lots[step + 1]):
                    max_job(m, head_banks[m % 2], m % 8, m // 8)

            copy_transposed(0, 0)
            project(0, True)
            with dve.Fori(1, HEAD_PAIR) as it:
                st.shift = (it - 1) * PER_PAIR
                n0 = st.n
                project(it, True)
                assert st.n - n0 == PER_PAIR
            st.shift = (HEAD_PAIR - 2) * PER_PAIR
            for it in range(HEAD_PAIR, NCHUNK // 2):
                project(it, it < NCHUNK // 2 - 1, head_jobs)
            make_shift(HEAD_JOBS - 2)
            for a in range(2):
                shift_job(HEAD_JOBS - 2 + a, head_banks[a], 0, a)

            PER_LOOP = 6
            def group(slot_of, base, i, s, first, last):
                p = 0
                if not first:
                    out_job(base, slot_of(0), i - 1)
                    p = 1
                if last:
                    return
                for m in range(HEAD_JOBS - 2):
                    max_job(base + p, slot_of(p), m % 8, m // 8)
                    p += 1
                make_shift(base + p)
                for a in range(2):
                    shift_job(base + p, slot_of(p), 1 - s, a)
                    p += 1

            base = HEAD_JOBS
            group(lambda p: side[(p + 2) % 3], base, 0, 0, True, False)
            base = 2 * HEAD_JOBS
            n0 = st.n
            n_shift = st.shift
            with dve.Fori(0, (NG - 2) // 2) as it:
                st.shift = it * PER_LOOP + n_shift
                group(lambda p: side[p % 3], it * (2 * BODY_JOBS) + base, it * 2 + 1, 1, False, False)
                group(lambda p: side[(BODY_JOBS + p) % 3], it * (2 * BODY_JOBS) + (base + BODY_JOBS), it * 2 + 2, 0, False, False)
                assert st.n - n0 == PER_LOOP, st.n - n0
            st.shift = n_shift + ((NG - 2) // 2 - 1) * PER_LOOP
            base = 2 * HEAD_JOBS + (NG - 2) * BODY_JOBS
            group(lambda p: side[p % 3], base, NG - 1, 1, False, True)
            out_job(base + 1, side[1], NG - 1)

            dve.wait_ge(s_ot, 1)
            for k in range(KT):
                v.tensor_scalar(oT[:, k, :], banks[k][:, :], bv[:, k:k + 1], None, ALU.add).then_inc(s_otc, 1)
            dve.wait_ge(s_y, 1)
            for i in range(TT):
                v.tensor_tensor(x1[:, i, :], score_a[:, i, :], x1[:, i, :], ALU.add).then_inc(t["s_x1"], 1)

        @block.tensor
        def _(pe):
            pe.wait_ge(s_id, 3)
            pe.wait_ge(s_xn, TT)
            for k in range(KT):
                for i in range(TT):
                    mm = pe.transpose(banks[k][:, i * P:(i + 1) * P], xn[:, i, k * P:(k + 1) * P], ident[:, :])
            mm.then_inc(s_xt, 1)
            pe.wait_ge(s_xts, KT)
            pe.wait_ge(s_w, LOADS * 16)
            for h in range(KT):
                for k in range(KT):
                    mm = pe.matmul(banks[2 + h][:, :], wq[:, k, h * P:(h + 1) * P], xT[:, k, :],
                                   start=(k == 0), stop=(k == KT - 1))
            mm.then_inc(s_qp, 1)

            def transposes(n, s, uses):
                pe.wait_ge(s_ctx[s], 16 * (uses + 1))
                wait_past(pe, s_tc, n * KT)
                for k in range(KT):
                    for j in range(CT):
                        mm = pe.transpose(banks[k][:, j * P:(j + 1) * P], ctx_in[s][:, j, k * P:(k + 1) * P], ident[:, :])
                mm.then_inc(s_tp, 1)

            def max_job(free, bank, s, m):
                k, c = m % 8, m // 8
                if free is not None:
                    pe.wait_ge(s_jd, free)
                pe.matmul(bank, qst[s][0:STACK, k // 2, (k % 2) * P:(k % 2 + 1) * P],
                          kst[s][0:STACK, k // 2, c * CHUNK:(c + 1) * CHUNK], start=True, stop=True).then_inc(s_job, 1)

            def project(it, more, head=False):
                for s in range(2):
                    n = it * 2 + s
                    todo = list(range(*head_range(n))) if head else []

                    def head_job():
                        if todo:
                            m = todo.pop(0)
                            if m == 0:
                                pe.wait_ge(s_q[0], 16)
                            if m % 16 == 0:
                                pe.wait_ge(s_kq[0][m // 16], 48)
                            max_job(m - 1 if m >= 2 else None, head_banks[m % 2], 0, m)

                    if more or s == 0:
                        transposes(n + 1, 1 - s, it + s)
                    pe.wait_ge(s_tc, n * KT + KT)
                    wait_past(pe, s_kf, n * KT)
                    for h in range(KT):
                        for k in range(KT):
                            mm = pe.matmul(banks[2 + h][:, :], wk[:, k, h * P:(h + 1) * P], ctxT[s][:, k, :],
                                           start=(k == 0), stop=(k == KT - 1))
                            if k == KT - 1:
                                mm.then_inc(s_kp, 1)
                            head_job()
                    wait_past(pe, s_vr, n)
                    for j in range(CT):
                        for k in range(KT):
                            mm = pe.matmul(score_a[:, j, :], ctxT[s][:, k, j * P:(j + 1) * P], wv[:, k, :],
                                           start=(k == 0), stop=(k == KT - 1))
                            if j == CT - 1 and k == KT - 1:
                                mm.then_inc(s_vp, 1)
                            head_job()
                    assert not todo

            pe.wait_ge(s_qf, KT)
            transposes(0, 0, 0)
            project(0, True)
            with pe.Fori(1, HEAD_PAIR) as it:
                project(it, True)
            for it in range(HEAD_PAIR, NCHUNK // 2):
                project(it, it < NCHUNK // 2 - 1, True)

            def shift_job(free, slot, a):
                pe.wait_ge(s_jd, free)
                for m in range(4):
                    mm = pe.matmul(slot[STACK:STACK + 2, m * P:(m + 1) * P], shift[:, 4 * a + m, :],
                                   identb[:, :], start=True, stop=True)
                mm.then_inc(s_job, 1)

            def out_job(free, slot, copied):
                pe.wait_ge(s_jd, free)
                pe.wait_ge(s_af, copied)
                for q in range(2):
                    mm = pe.transpose(slot[:, q * P:(q + 1) * P], acc_s[:, q * P:(q + 1) * P], ident[:, :])
                mm.then_inc(s_job, 1)

            def unit_scores(s, n, u):
                if n is not None:
                    pe.wait_ge(s_ex, n - 1)
                for j in range(HG):
                    mm = pe.matmul((score_a, score_b)[u % 2][:, j, :], kst[s][:, j, u * P:(u + 1) * P],
                                   qst[s][:, j, :], start=True, stop=True)
                mm.then_inc(s_sc, 1)

            def unit_values(s, n, u):
                pe.wait_ge(s_ex, n + 1)
                for j in range(HG):
                    mm = pe.matmul(acc[32 * j:32 * j + D + 1, :], vg[s][:, u, j, :], probs[u % len(probs)][:, j, :],
                                   start=(u == 0), stop=(u == UNITS - 1))
                mm.then_inc(s_pf, 1)

            def group(slot_of, base, free, i, s, uses, first, last):
                p = 0
                for u in range(UNITS):
                    n = i * UNITS + u
                    if u + 2 < UNITS:
                        unit_scores(s, n + 2 if not first or u > 0 else n + 2, u + 2)
                    elif not last:
                        if u + 2 == UNITS:
                            pe.wait_ge(s_jd, base + p)
                        unit_scores(1 - s, n + 2, u + 2 - UNITS)
                    if u == 0:
                        pe.wait_ge(s_vg[s], 16 * (uses + 1))
                        pe.wait_ge(s_af, i)
                    unit_values(s, n, u)
                    if u == 1 and not first:
                        out_job(free(0), slot_of(0), i)
                        p = 1
                    if last:
                        continue
                    for m in max_jobs_at(u):
                        nxt = uses + (1 if s == 1 else 0)
                        if m == 0:
                            pe.wait_ge(s_q[1 - s], 16 * (nxt + 1))
                        if m % 16 == 0:
                            pe.wait_ge(s_kq[1 - s][m // 16], 48 * (nxt + 1))
                        max_job(free(p), slot_of(p), 1 - s, m)
                        p += 1
                    if u == LAST_T + 2:
                        pe.wait_ge(s_sh, i + 2)
                        for a in range(2):
                            shift_job(free(p), slot_of(p), a)
                            p += 1

            pe.wait_ge(s_sh, 1)
            for a in range(2):
                shift_job(HEAD_JOBS - 2, head_banks[a], a)
            pe.wait_ge(s_jd, HEAD_JOBS)
            pe.wait_ge(s_ones, 4)
            pe.wait_ge(s_kf, NCHUNK * KT)
            pe.wait_ge(s_vr, NCHUNK)
            for u in range(2):
                unit_scores(0, None, u)
            group(lambda p: side[(p + 2) % 3], HEAD_JOBS, lambda p: HEAD_JOBS + p - 2, 0, 0, 0, True, False)
            with pe.Fori(0, (NG - 2) // 2) as it:
                base = it * (2 * BODY_JOBS) + 2 * HEAD_JOBS
                group(lambda p: side[p % 3], base, lambda p: free_job(p, base), it * 2 + 1, 1, it, False, False)
                group(lambda p: side[(BODY_JOBS + p) % 3], base + BODY_JOBS, lambda p: base + (BODY_JOBS + p - 2),
                      it * 2 + 2, 0, it + 1, False, False)
            base = 2 * HEAD_JOBS + (NG - 2) * BODY_JOBS
            group(lambda p: side[p % 3], base, lambda p: free_job(p, base), NG - 1, 1, (NG - 2) // 2, False, True)
            out_job(base, side[1], NG)

            pe.wait_ge(s_jd, base + 2)
            for k in range(KT):
                for i in range(TT):
                    b, q = i // 2, i % 2
                    rows = o[:, q, b * GROUPS + 2 * k:b * GROUPS + 2 * k + 2, :, :].rearrange("p g j d -> p (g j d)")
                    mm = pe.transpose(banks[k][:, i * P:(i + 1) * P], rows, ident[:, :])
            mm.then_inc(s_ot, 1)
            pe.wait_ge(s_otc, KT)
            for i in range(TT):
                for k in range(KT):
                    mm = pe.matmul(score_a[:, i, :], oT[:, k, i * P:(i + 1) * P], wo[:, k, :],
                                   start=(k == 0), stop=(k == KT - 1))
            mm.then_inc(s_y, 1)


def latent_attention(nc, t):
    T = NQ
    RQ, RK, RD = 128, 64, 32
    HS = 64
    HD = RD + D
    HV = P // HG
    PAIRS = H // 2
    SCALE = float(1.0 / np.sqrt(np.float32(HD)))
    with ExitStack() as ctx:
        def sb(name, shape, dt=F32):
            return ctx.enter_context(nc.sbuf_tensor(name, shape, dt))

        def sem(name):
            return ctx.enter_context(nc.semaphore(name))

        units = [(b, q, g) for b in range(B) for g in range(H // HG) for q in range(2)]
        x1, ident, identb = t["x1"], t["ident"], t["identb"]
        w = t["attn_w"]
        stats = sb("a_stats", [P, TT, 6])
        mv = sb("a_mv", [P, TT, 2])
        sd = sb("a_sd", [P, TT, 2])
        xn = sb("a_xn", [P, TT, C])
        xT = sb("a_xT", [P, KT, TOK])
        qcT = sb("qcT", [RQ, TOK])
        kv = sb("kv", [P, TT, RK])
        kv2 = sb("kv2", [P, TT, RK])
        ms = sb("ms", [P, TT])
        rms = sb("rms", [P, TT])
        kvT = sb("kvT", [RK, TOK])
        rot = sb("rot", [P, 2, H, RD])
        q_rows = sb("q_rows", [P, TT, H, HS])
        k_rows = sb("k_rows", [P, TT, H, HS])
        v_rows = sb("va_rows", [P, TT, H, HV])
        wo = sb("a_wo", [P, H // HG, C])
        qT = sb("qT", [P, PAIRS, TOK])
        kT = sb("kT", [P, PAIRS, TOK])
        diag = sb("diag", [P, P], BF16)
        zeros = sb("zeros", [P, C])
        pr = [sb(f"pr{i}", [P, HG, T]) for i in range(2)]
        prT = [sb(f"prT{i}", [P, HG, 2, P]) for i in range(2)]
        top = sb("a_top", [P, 2, HG])
        ntop = sb("a_ntop", [P, 2, HG])
        rtot = sb("a_rtot", [P, T])
        pick = sb("pick", [P, HG, HV])
        oT = q_rows[:, 0:2, :, :].rearrange("p a h d -> p (a h d)").rearrange("p (g n) -> p g n", g=H // HG)
        pairs = [ctx.enter_context(nc.psum_tensor(f"a_bank{i}", [P, 2, 512], F32)) for i in range(4)]
        vbank = [pairs[i // 2][:, i % 2, :] for i in range(4)]
        abank = [pairs[2 + i // 2][:, i % 2, :] for i in range(4)]

        s_st = sem("a_steps")
        s_var = sem("a_variance_ready")
        s_sd = sem("a_deviation_ready")
        s_xn = sem("a_normed_ready")
        s_vw = sem("a_vector_bank_written")
        s_vr = sem("a_vector_bank_read")
        s_aw = sem("a_scalar_bank_written")
        s_ar = sem("a_scalar_bank_read")
        s_ms = sem("a_mean_square_ready")
        s_rms = sem("a_rms_ready")
        s_kvn = sem("a_latent_normed")
        s_pad = sem("a_padding_ready")
        s_qr = sem("a_query_rotated")
        s_qr2 = sem("a_query_content_copied")
        s_kr = sem("a_key_rotated")
        s_s = sem("a_scores_ready")
        s_nt = sem("a_maxima_ready")
        s_p = sem("a_probs_ready")
        s_t = sem("a_probs_transposed")
        s_tc = sem("a_probs_transposed_copied")
        s_ps = sem("a_sums_spread")
        s_on = sem("a_output_normed")
        s_o = sem("a_output_ready")
        s_oc = sem("a_output_copied")
        s_wo = sem("a_out_weights_in")
        s_y = sem("a_out_product")

        NU = len(units)
        block = ctx.enter_context(nc.Block())

        @block.sync
        def _(sp):
            for dst, src in t["ffn_small"]:
                sp.dma_start(dst, src).then_inc(t["s_fw"], 16)
            for e in range(E):
                sp.dma_start(t["b2"][:, e, :], t["b2_in"][e, :].partition_broadcast(P)).then_inc(t["s_fw"], 16)
                sp.dma_start(t["w2"][:, e * FT:(e + 1) * FT, :], t["w2_in"][e, :, :].rearrange("(f p) c -> p f c", p=P)).then_inc(t["s_fw"], 16)
            sp.wait_ge(s_pad, 9)
            for j in range(HG):
                sp.dma_start(wo[j * HV:j * HV + D, :, :], t["attn_wo"].rearrange("(g j d) c -> j d g c", j=HG, d=D)[j, :, :, :]).then_inc(s_wo, 16)
            sp.dma_start(t["slots"].rearrange("(t p) c -> p t c", p=P),
                         zeros[:].unsqueeze(1).to_broadcast([P, TILES, C])).then_inc(t["s_zero"], 16)
            sp.wait_ge(t["s_fw"], 16 * t["n_fw"])
            sp.wait_ge(t["s_zero"], 16)
            sp.wait_ge(s_wo, HG * 16)

        @block.gpsimd
        def _(eng):
            eng.memset(q_rows[:], 0.0).then_inc(s_pad, 1)
            eng.memset(k_rows[:], 0.0).then_inc(s_pad, 1)
            eng.memset(diag[:], 0.0).then_inc(s_pad, 1)
            eng.memset(v_rows[:], 0.0).then_inc(s_pad, 1)
            eng.wait_ge(s_pad, 4)
            eng.memset(v_rows[:, :, :, D:D + 1], 1.0).then_inc(s_pad, 1)
            eng.affine_select(out=diag[:], in_=diag[:], compare_op=ALU.is_ge, fill=-1.0e30,
                              base=0, pattern=[[-1, P]], channel_multiplier=1).then_inc(s_pad, 1)
            eng.memset(zeros[:], 0.0).then_inc(s_pad, 1)
            eng.memset(wo[:], 0.0).then_inc(s_pad, 1)
            eng.memset(pick[:], 0.0).then_inc(s_pad, 1)
            eng.wait_ge(s_pad, 9)
            eng.affine_select(out=pick[:], in_=pick[:], compare_op=ALU.not_equal, fill=1.0,
                              base=-D, pattern=[[-HV, HG], [0, HV]], channel_multiplier=1).then_inc(s_pad, 1)

        @block.vector
        def _(dve):
            st = Steps(dve, s_st)
            v = nc.vector
            job = [0]

            def vjob():
                job[0] += 1
                dve.wait_ge(s_vw, job[0])
                return vbank[(job[0] - 1) % 4]

            for i in range(TT):
                last = st.mark(v.bn_stats(stats[:, i, :], x1[:, i, :]))
            dve.wait_ge(s_st, last)
            for i in range(TT):
                last = st.mark(v.bn_aggr(mv[:, i, :], stats[:, i, :]))
            dve.wait_ge(s_st, last)
            v.tensor_scalar(sd[:, :, 0], mv[:, :, 1], LN_EPS, None, ALU.add).then_inc(s_var, 1)
            dve.wait_ge(s_sd, 1)
            st.link(v.reciprocal(sd[:, :, 0], sd[:, :, 1]))
            for i in range(TT):
                v.tensor_scalar(xn[:, i, :], x1[:, i, :], mv[:, i, 0:1], sd[:, i, 0:1],
                                ALU.subtract, ALU.mult).then_inc(s_xn, 1)
            for k in range(KT):
                v.tensor_copy(xT[:, k, :], vjob()).then_inc(s_vr, 1)

            bank = vjob()
            v.tensor_copy(kv[:].rearrange("p a c -> p (a c)"), bank[:, 0:TT * RK]).then_inc(s_vr, 1)
            dve.wait_ge(s_vr, job[0])
            st.link(v.tensor_tensor(kv2[:], kv[:], kv[:], ALU.mult))
            st.link(v.reduce_sum(ms[:], kv2[:], AXX))
            v.tensor_scalar(rms[:], ms[:], 1.0 / RK, 1e-6, ALU.mult, ALU.add).then_inc(s_ms, 1)

            dve.wait_ge(s_pad, 4)

            def rotate(rows, i, done):
                bank = vjob().rearrange("p (h d) -> p h d", d=RD)
                cos = w["cos"][:, i % 2, :].unsqueeze(1)
                sin = w["sin"][:, i % 2, :].unsqueeze(1)
                h2 = RD // 2
                if job[0] > 4:
                    dve.wait_ge(s_st, st.n)
                a = st.mark(v.tensor_tensor(rot[:, 0, :, :], bank, cos.to_broadcast([P, H, RD]), ALU.mult))
                v.tensor_tensor(rot[:, 1, :, 0:h2], bank[:, :, h2:RD], sin[:, :, 0:h2].to_broadcast([P, H, h2]), ALU.mult).then_inc(s_st, 1)
                st.n += 1
                v.tensor_tensor(rot[:, 1, :, h2:RD], bank[:, :, 0:h2], sin[:, :, h2:RD].to_broadcast([P, H, h2]), ALU.mult).then_inc(s_vr, 1)
                dve.wait_ge(s_vr, job[0])
                dve.wait_ge(s_st, st.n)
                v.tensor_tensor(rows[:, i, :, 0:RD], rot[:, 0, :, :], rot[:, 1, :, :], ALU.add).then_inc(done, 1)
                dve.wait_ge(done, i + 1)

            for i in range(TT):
                rotate(k_rows, i, s_kr)
            dve.wait_ge(s_rms, 1)
            st.link(v.reciprocal(ms[:], rms[:]))
            v.tensor_tensor(kv2[:], kv[:], ms[:].unsqueeze(2).to_broadcast([P, TT, RK]), ALU.mult).then_inc(s_kvn, 1)
            for i in range(TT):
                rotate(q_rows, i, s_qr)
            bank = vjob()
            v.tensor_scalar(kvT[:], bank[0:RK, :], w["g"][:, 0:1], None, ALU.mult).then_inc(s_vr, 1)
            for i in range(TT):
                for h in range(2):
                    v.tensor_copy(qT[:, 4 * h:4 * h + 4, i * P:(i + 1) * P],
                                  vjob().rearrange("p (a n) -> p a n", a=4)).then_inc(s_vr, 1)

            def maxima(u):
                b, q, g = units[u]
                n = P * (q + 1)
                dve.wait_ge(s_s, u + 1)
                if u >= 2:
                    dve.wait_ge(s_p, u - 1)
                rows = pairs[u % 2][:].rearrange("p a (c n) -> p c a n", c=2)
                st.link(v.reduce_max(top[:, u % 2, :].rearrange("p (c a) -> p c a", a=2), rows[:, :, :, 0:n], AXX))
                v.tensor_scalar(ntop[:, u % 2, :], top[:, u % 2, :], -SCALE, None, ALU.mult).then_inc(s_nt, 1)

            def copy_output(m):
                b, q, g = units[2 * m]
                dve.wait_ge(s_o, 2 * m + 2)
                v.tensor_copy(oT[:, g, b * T:(b + 1) * T], pairs[3][:, m % 2, 0:T]).then_inc(s_oc, 1)

            def norm_output(m):
                b, q, g = units[2 * m]
                dve.wait_ge(s_ps, m + 1)
                st.link(v.reciprocal(rtot[:], pairs[3][:, m % 2, T:2 * T]))
                rows = oT[:, g, b * T:(b + 1) * T]
                v.tensor_tensor(rows, rows, rtot[:], ALU.mult).then_inc(s_on, 1)

            maxima(0)
            maxima(1)
            for u in range(NU):
                if u + 2 < NU:
                    maxima(u + 2)
                if u >= 2 and u % 2 == 0:
                    copy_output(u // 2 - 1)
                if u >= 2 and u % 2 == 1:
                    norm_output(u // 2 - 1)
            copy_output(NU // 2 - 1)
            norm_output(NU // 2 - 1)

            dve.wait_ge(s_y, 1)
            for i in range(TT):
                v.tensor_tensor(x1[:, i, :], pairs[1 + i // 2][:].rearrange("p a c -> p (a c)")[:, (i % 2) * C:(i % 2 + 1) * C],
                                x1[:, i, :], ALU.add).then_inc(t["s_x2"], 1)

        @block.scalar
        def _(act):
            job = [0]

            def ajob():
                job[0] += 1
                act.wait_ge(s_aw, job[0])
                return abank[(job[0] - 1) % 4]

            act.wait_ge(s_var, 1)
            act.activation(sd[:, :, 1], sd[:, :, 0], ACT.Sqrt).then_inc(s_sd, 1)
            act.activation(qcT[:], ajob(), ACT.Copy).then_inc(s_ar, 1)
            act.wait_ge(s_ms, 1)
            act.activation(rms[:], rms[:], ACT.Sqrt).then_inc(s_rms, 1)
            act.wait_ge(s_pad, 4)
            for i in range(TT):
                bank = ajob()
                act.activation(q_rows[:, i, :, RD:HD], bank[:, 0:C].rearrange("p (h d) -> p h d", d=D), ACT.Copy).then_inc(s_qr2, 1)
                act.activation(k_rows[:, i, :, RD:HD], bank[:, C:2 * C].rearrange("p (h d) -> p h d", d=D), ACT.Copy).then_inc(s_ar, 1)
                act.activation(v_rows[:, i, :, 0:D], ajob()[:, 0:C].rearrange("p (h d) -> p h d", d=D), ACT.Copy).then_inc(s_ar, 1)
            for i in range(TT):
                for h in range(2):
                    act.activation(kT[:, 4 * h:4 * h + 4, i * P:(i + 1) * P],
                                   ajob().rearrange("p (a n) -> p a n", a=4), ACT.Copy).then_inc(s_ar, 1)

            def probabilities(u):
                b, q, g = units[u]
                n = P * (q + 1)
                act.wait_ge(s_nt, u + 1)
                if u >= 2:
                    act.wait_ge(s_t, u - 1)
                for j in range(HG):
                    c = (j // 2) * T
                    ins = act.activation(pr[u % 2][:, j, 0:n], pairs[u % 2][:, j % 2, c:c + n], ACT.Exp, bias=ntop[:, u % 2, j:j + 1],
                                         scale=SCALE)
                ins.then_inc(s_p, 1)

            def copy_probs(u):
                b, q, g = units[u]
                act.wait_ge(s_t, u + 1)
                if u >= 2:
                    act.wait_ge(s_o, u - 1)
                act.activation(prT[u % 2][:, :, 0:q + 1, :],
                               pairs[2][:].rearrange("p a c -> p (a c)").rearrange("p (j k n) -> p j k n", j=HG, k=2)[:, :, 0:q + 1, :],
                               ACT.Copy).then_inc(s_tc, 1)

            probabilities(0)
            for u in range(NU):
                if u + 1 < NU:
                    probabilities(u + 1)
                copy_probs(u)

        @block.tensor
        def _(pe):
            nv, na = [0], [0]

            def vring():
                nv[0] += 1
                if nv[0] > 4:
                    pe.wait_ge(s_vr, nv[0] - 4)
                return vbank[(nv[0] - 1) % 4]

            def aring():
                na[0] += 1
                if na[0] > 4:
                    pe.wait_ge(s_ar, na[0] - 4)
                return abank[(na[0] - 1) % 4]

            pe.wait_ge(s_xn, TT)
            for k in range(KT):
                bank = vring()
                for i in range(TT):
                    mm = pe.transpose(bank[:, i * P:(i + 1) * P], xn[:, i, k * P:(k + 1) * P], ident[:, :])
                mm.then_inc(s_vw, 1)
            pe.wait_ge(s_vr, KT)
            bank = aring()
            for k in range(KT):
                mm = pe.matmul(bank, w["wq"][:, k, :], xT[:, k, :], start=(k == 0), stop=(k == KT - 1))
            mm.then_inc(s_aw, 1)
            bank = vring()
            for i in range(TT):
                for k in range(KT):
                    mm = pe.matmul(bank[:, i * RK:(i + 1) * RK], xT[:, k, i * P:(i + 1) * P], w["wkv"][:, k, :],
                                   start=(k == 0), stop=(k == KT - 1))
            mm.then_inc(s_vw, 1)
            for i in range(TT):
                bank = vring()
                for k in range(KT):
                    mm = pe.matmul(bank, xT[:, k, i * P:(i + 1) * P], w["wkr"][:, k, :], start=(k == 0), stop=(k == KT - 1))
                mm.then_inc(s_vw, 1)
            pe.wait_ge(s_ar, 1)
            for i in range(TT):
                pe.matmul(vring(), qcT[:, i * P:(i + 1) * P], w["wqr"][:, :], start=True, stop=True).then_inc(s_vw, 1)
            pe.wait_ge(s_kvn, 1)
            bank = vring()
            for i in range(TT):
                mm = pe.transpose(bank[0:RK, i * P:(i + 1) * P], kv2[:, i, :], ident[:, :])
            mm.then_inc(s_vw, 1)
            pe.wait_ge(s_vr, nv[0])
            for i in range(TT):
                bank = aring()
                pe.matmul(bank[:, 0:C], qcT[:, i * P:(i + 1) * P], w["wqd"][:, :], start=True, stop=True)
                pe.matmul(bank[:, C:2 * C], kvT[:, i * P:(i + 1) * P], w["wkd"][:, :], start=True, stop=True).then_inc(s_aw, 1)
                pe.matmul(aring()[:, 0:C], kvT[:, i * P:(i + 1) * P], w["wvd"][:, :], start=True, stop=True).then_inc(s_aw, 1)
            for i in range(TT):
                pe.wait_ge(s_qr, i + 1)
                pe.wait_ge(s_kr, i + 1)
                pe.wait_ge(s_qr2, i + 1)
                pe.wait_ge(s_ar, 3 + 2 * i)
                for h in range(2):
                    for rows, ring, s in ((q_rows, vring, s_vw), (k_rows, aring, s_aw)):
                        bank = ring()
                        for a in range(4):
                            c = 2 * (4 * h + a)
                            mm = pe.transpose(bank[:, a * P:(a + 1) * P],
                                              rows[:, i, c:c + 2, :].rearrange("p h d -> p (h d)"), ident[:, :])
                        mm.then_inc(s, 1)
            pe.wait_ge(s_vr, nv[0])
            pe.wait_ge(s_ar, na[0])
            pe.wait_ge(s_pad, 10)

            def unit_scores(u):
                b, q, g = units[u]
                n = P * (q + 1)
                i = 2 * b + q
                if u >= 2:
                    pe.wait_ge(s_p, u - 1)
                for j in range(HG):
                    h = g * HG + j
                    r = HS * (h % 2)
                    pe.matmul(pairs[u % 2][:, j % 2, (j // 2) * T:(j // 2) * T + n],
                              qT[r:r + HD, h // 2, i * P:(i + 1) * P], kT[r:r + HD, h // 2, b * T:b * T + n],
                              start=True, stop=False)
                    c = (j // 2) * T + q * P
                    mm = pe.matmul(pairs[u % 2][:, j % 2, c:c + P], identb[:, :], diag[:], start=False, stop=True)
                mm.then_inc(s_s, 1)

            def unit_transposes(u):
                b, q, g = units[u]
                pe.wait_ge(s_p, u + 1)
                if u >= 1:
                    pe.wait_ge(s_tc, u)
                for j in range(HG):
                    for k in range(q + 1):
                        c = (2 * j + k) * P
                        mm = pe.transpose(pairs[2][:].rearrange("p a c -> p (a c)")[:, c:c + P],
                                          pr[u % 2][:, j, k * P:(k + 1) * P], ident[:, :])
                mm.then_inc(s_t, 1)

            def unit_values(u):
                b, q, g = units[u]
                pe.wait_ge(s_tc, u + 1)
                m = u // 2
                if m >= 2:
                    pe.wait_ge(s_on, m - 1)
                for k in range(q + 1):
                    for j in range(HG):
                        mm = pe.matmul(pairs[3][j * HV:(j + 1) * HV, m % 2, q * P:(q + 1) * P], v_rows[:, 2 * b + k, g * HG + j, :],
                                       prT[u % 2][:, j, k, :], start=(k == 0), stop=(k == q))
                mm.then_inc(s_o, 1)

            def spread_sums(m):
                b, q, g = units[2 * m]
                pe.wait_ge(s_oc, m + 1)
                pe.matmul(pairs[3][:, m % 2, T:2 * T], pick[:].rearrange("p j e -> p (j e)"), oT[:, g, b * T:(b + 1) * T],
                          start=True, stop=True).then_inc(s_ps, 1)

            unit_scores(0)
            unit_scores(1)
            unit_transposes(0)
            for u in range(NU):
                if u + 2 < NU:
                    unit_scores(u + 2)
                if u + 1 < NU:
                    unit_transposes(u + 1)
                unit_values(u)
                if u >= 2 and u % 2 == 1:
                    spread_sums(u // 2 - 1)
            spread_sums(NU // 2 - 1)

            pe.wait_ge(s_on, NU // 2)
            pe.wait_ge(s_wo, HG * 16)
            for i in range(TT):
                for g in range(H // HG):
                    mm = pe.matmul(pairs[1 + i // 2][:].rearrange("p a c -> p (a c)")[:, (i % 2) * C:(i % 2 + 1) * C],
                                   oT[:, g, i * P:(i + 1) * P], wo[:, g, :], start=(g == 0), stop=(g == H // HG - 1))
            mm.then_inc(s_y, 1)


def expert_layer(nc, t, out):
    with ExitStack() as ctx:
        def sb(name, shape, dt=F32):
            return ctx.enter_context(nc.sbuf_tensor(name, shape, dt))

        def ps(name, shape):
            return ctx.enter_context(nc.psum_tensor(name, shape, F32))

        def sem(name):
            return ctx.enter_context(nc.semaphore(name))

        x2, ident, w2, b1, b2, rw, rb, cst = (t[n] for n in ("x1", "ident", "w2", "b1", "b2", "rw", "rb", "cst"))
        slots, y_slots = t["slots"], nc.dram_tensor("y_slots", [TILES * P, C], F32).ap()
        stats = sb("f_stats", [P, TT, 6])
        mv = sb("f_mv", [P, TT, 2])
        sd = sb("f_sd", [P, TT, 2])
        xn = sb("f_xn", [P, TT, C])
        xT = sb("f_xT", [P, KT, TOK])
        logit = sb("logit", [P, TT, E])
        less = sb("less", [P, TT, E])
        ex = sb("ex", [P, TT, E])
        best = sb("best", [P, TT])
        esum = sb("esum", [P, TT])
        gate = sb("gate", [P, TT])
        tie = sb("tie", [P, TT, E])
        first = sb("first", [P, TT])
        chosen = sb("chosen", [P, TT, E])
        chosenb = sb("chosenb", [P, TT, E], BF16)
        upper = sb("upper", [P, P], BF16)
        onesb = sb("onesb", [P, P], BF16)
        over = sb("over", [P, E, TT])
        tiles = sb("tiles", [P, E])
        before = sb("before", [P, E, E])
        start = sb("start", [P, E])
        end = sb("end", [P, E])
        place = sb("place", [P, TT, E])
        slot = sb("slot", [P, TT])
        slot_u = sb("slot_u", [P, TT], mybir.dt.uint32)
        done = sb("done", [P, TILES, E])
        expert = sb("expert", [P, TILES])
        expert_i = sb("expert_i", [P, TILES], mybir.dt.int32)
        xs = sb("xs", [P, TILES, C])
        xsT = sb("xsT", [P, TILES, KT, P])
        w1 = [sb(f"w1_{i}", [P, KT, F]) for i in range(2)]
        hT = [sb(f"hT{i}", [P, FT, P]) for i in range(2)]
        ys = [sb(f"ys{i}", [P, C]) for i in range(2)]
        yg = sb("yg", [P, TT, C])
        bank = [ps(f"f_bank{i}", [P, 512]) for i in range(2)]
        hp = [ps(f"h_bank{i}", [P, FT, P]) for i in range(2)]
        yp = [ps(f"y_bank{i}", [P, C]) for i in range(2)]

        s_st = sem("f_steps")
        s_var = sem("f_variance_ready")
        s_sd = sem("f_deviation_ready")
        s_xn = sem("f_normed_ready")
        s_xt = sem("f_transposed")
        s_xts = sem("f_transposed_copied")
        s_lg = sem("logits_ready")
        s_ls = sem("logits_shifted")
        s_ex = sem("logits_exp_ready")
        s_c = sem("choice_ready")
        s_tri = sem("triangle_ready")
        s_rk = sem("ranks_ready")
        s_slot = sem("slots_ready")
        s_te = sem("tile_experts_ready")
        s_sc = sem("rows_scattered")
        s_xs = sem("slot_rows_in")
        s_st_t = sem("slot_rows_transposed")
        s_st_c = sem("slot_rows_copied")
        s_w1 = [sem(f"w1_in_{i}") for i in range(2)]
        s_h = sem("hidden_product")
        s_hr = sem("hidden_ready")
        s_y = sem("tile_product")
        s_ys = sem("tile_rows_ready")
        s_yo = [sem(f"tile_rows_stored_{i}") for i in range(2)]
        s_yg = sem("rows_gathered")
        s_f = sem("final_rows_ready")
        s_out = sem("out_stored")
        block = ctx.enter_context(nc.Block())

        def expert_of(eng, tile):
            return eng.value_load(expert_i[0:1, bass.ds(tile, 1)], min_val=0, max_val=E - 1)

        @block.gpsimd
        def _(eng):
            eng.memset(onesb[:], 1.0).then_inc(s_tri, 1)
            eng.wait_ge(s_tri, 1)
            eng.affine_select(out=upper[:], in_=onesb[:], compare_op=ALU.is_gt, fill=0.0,
                              base=0, pattern=[[1, P]], channel_multiplier=-1).then_inc(s_tri, 1)
            eng.wait_ge(s_slot, 1)
            eng.wait_ge(t["s_zero"], 16)
            for i in range(TT):
                eng.indirect_dma_start(slots, bass.IndirectOffsetOnAxis(ap=slot_u[:, i:i + 1], axis=0), xn[:, i, :], None).then_inc(s_sc, 16)
            for i in range(2):
                eng.wait_ge(s_yo[i], 16 * ((TILES + 1 - i) // 2))
            for i in range(TT):
                eng.indirect_dma_start(yg[:, i, :], None, y_slots, bass.IndirectOffsetOnAxis(ap=slot_u[:, i:i + 1], axis=0)).then_inc(s_yg, 16)

        @block.sync
        def _(sp):
            def load_w1(s, tile):
                e = expert_of(sp, tile)
                sp.dma_start(w1[s][:], t["w1_in"][bass.ds(e, 1), :, :].rearrange("o (k p) n -> p (o k) n", p=P)).then_inc(s_w1[s], 16)

            def store(s, tile):
                sp.wait_ge(s_ys, tile + 1)
                sp.dma_start(y_slots[bass.ds(tile * P, P), :], ys[s][:]).then_inc(s_yo[s], 16)

            sp.wait_ge(s_te, 1)
            for i in range(2):
                load_w1(i, i)
            sp.wait_ge(s_sc, 16 * TT)
            sp.dma_start(xs[:], slots.rearrange("(t p) c -> p t c", p=P)).then_inc(s_xs, 16)
            with sp.Fori(0, (TILES - 3) // 2) as it:
                for s in range(2):
                    tile = it * 2 + s
                    sp.wait_ge(s_h, tile + 1)
                    load_w1(s, tile + 2)
                    store(s, tile)
            sp.wait_ge(s_h, TILES - 2)
            load_w1(0, TILES - 1)
            for n in range(TILES - 3, TILES):
                store(n % 2, n)
            sp.wait_ge(s_f, TT)
            sp.dma_start(out.rearrange("b (q p) c -> p (b q) c", p=P), x2[:]).then_inc(s_out, 16)
            sp.wait_ge(s_out, 16)

        @block.vector
        def _(dve):
            st = Steps(dve, s_st)
            v = nc.vector
            for i in range(TT):
                last = st.mark(v.bn_stats(stats[:, i, :], x2[:, i, :]))
            dve.wait_ge(s_st, last)
            for i in range(TT):
                last = st.mark(v.bn_aggr(mv[:, i, :], stats[:, i, :]))
            dve.wait_ge(s_st, last)
            v.tensor_scalar(sd[:, :, 0], mv[:, :, 1], LN_EPS, None, ALU.add).then_inc(s_var, 1)
            dve.wait_ge(s_sd, 1)
            st.link(v.reciprocal(sd[:, :, 0], sd[:, :, 1]))
            for i in range(TT):
                v.tensor_scalar(xn[:, i, :], x2[:, i, :], mv[:, i, 0:1], sd[:, i, 0:1],
                                ALU.subtract, ALU.mult).then_inc(s_xn, 1)
            dve.wait_ge(s_xt, 1)
            for k in range(KT):
                v.tensor_copy(xT[:, k, :], bank[k][:, :]).then_inc(s_xts, 1)

            dve.wait_ge(t["s_fw"], 16 * t["n_fw"])
            dve.wait_ge(s_lg, 1)
            st.link(v.tensor_tensor(logit[:], bank[0][:, 0:TT * E].rearrange("p (i e) -> p i e", e=E),
                                    rb[:].unsqueeze(1).to_broadcast([P, TT, E]), ALU.add))
            st.link(v.reduce_max(best[:], logit[:], AXX))
            high = best[:].unsqueeze(2).to_broadcast([P, TT, E])
            v.tensor_tensor(less[:], logit[:], high, ALU.subtract).then_inc(s_ls, 1)
            st.link(v.tensor_tensor(tie[:], logit[:], high, ALU.is_ge))
            st.link(v.tensor_tensor(tie[:], tie[:], cst["fall"].unsqueeze(1).to_broadcast([P, TT, E]), ALU.mult))
            st.link(v.reduce_max(first[:], tie[:], AXX))
            st.link(v.tensor_tensor(chosen[:], tie[:], first[:].unsqueeze(2).to_broadcast([P, TT, E]), ALU.is_equal))
            v.tensor_copy(chosenb[:], chosen[:]).then_inc(s_c, 1)
            dve.wait_ge(s_ex, 1)
            st.link(v.reduce_sum(esum[:], ex[:], AXX))
            st.link(v.reciprocal(gate[:], esum[:]))

            dve.wait_ge(s_rk, 1)
            ranks = bank[1][:, 0:TT * E].rearrange("p (i e) -> p i e", e=E)
            counts = bank[1][:, TT * E:(TT + 1) * E]
            st.link(v.tensor_tensor(over[:], counts.unsqueeze(2).to_broadcast([P, E, TT]),
                                    cst["fill"].unsqueeze(1).to_broadcast([P, E, TT]), ALU.is_gt))
            st.link(v.reduce_sum(tiles[:], over[:], AXX))
            st.link(v.tensor_tensor(before[:], tiles[:].unsqueeze(1).to_broadcast([P, E, E]),
                                    cst["lower"].rearrange("p (a b) -> p a b", b=E), ALU.mult))
            st.link(v.reduce_sum(start[:], before[:], AXX))
            st.link(v.scalar_tensor_tensor(out=place[:], in0=start[:].unsqueeze(1).to_broadcast([P, TT, E]), scalar=float(P),
                                           in1=ranks, op0=ALU.mult, op1=ALU.add))
            st.link(v.tensor_tensor(place[:], place[:], chosen[:], ALU.mult))
            st.link(v.reduce_sum(slot[:], place[:], AXX))
            v.tensor_copy(slot_u[:], slot[:]).then_inc(s_slot, 1)
            st.link(v.tensor_tensor(end[:], start[:], tiles[:], ALU.add))
            st.link(v.tensor_tensor(done[:], end[:].unsqueeze(1).to_broadcast([P, TILES, E]),
                                    cst["tile"].unsqueeze(2).to_broadcast([P, TILES, E]), ALU.is_le))
            st.link(v.reduce_sum(expert[:], done[:], AXX))
            v.tensor_scalar(expert_i[:], expert[:], float(E - 1), None, ALU.min).then_inc(s_te, 1)

            for n in range((TILES + 1) // 2):
                m = min(2, TILES - 2 * n)
                dve.wait_ge(s_st_t, n + 1)
                v.tensor_copy(xsT[:, 2 * n:2 * n + m, :, :].rearrange("p t k n -> p (t k n)"),
                              bank[n % 2][:, 0:m * C]).then_inc(s_st_c, 1)

            def tile_rows(s, tile, used):
                e = expert_of(dve, tile)
                dve.wait_ge(s_y, tile + 1)
                wait_past(dve, s_yo[s], 16 * used)
                v.tensor_tensor(ys[s][:].unsqueeze(1), yp[s][:].unsqueeze(1), b2[:, bass.ds(e, 1), :], ALU.add).then_inc(s_ys, 1)

            dve.wait_ge(s_te, 1)
            for s in range(2):
                tile_rows(s, s, 0)
            with dve.Fori(1, (TILES - 1) // 2) as it:
                for s in range(2):
                    tile_rows(s, it * 2 + s, it)
            tile_rows(0, TILES - 1, (TILES - 1) // 2)

            dve.wait_ge(s_yg, 16 * TT)
            for i in range(TT):
                v.scalar_tensor_tensor(out=x2[:, i, :], in0=yg[:, i, :], scalar=gate[:, i:i + 1], in1=x2[:, i, :],
                                       op0=ALU.mult, op1=ALU.add).then_inc(s_f, 1)

        @block.scalar
        def _(act):
            act.wait_ge(s_var, 1)
            act.activation(sd[:, :, 1], sd[:, :, 0], ACT.Sqrt).then_inc(s_sd, 1)
            act.wait_ge(s_ls, 1)
            act.activation(ex[:], less[:], ACT.Exp).then_inc(s_ex, 1)

            def hidden(s, tile):
                e = expert_of(act, tile)
                act.wait_ge(s_h, tile + 1)
                for f in range(FT):
                    act.activation(hT[s][:, f, :], hp[s][:, f, :], ACT.Relu,
                                   bias=b1[:, bass.ds(e * FT + f, 1)]).then_inc(s_hr, 1)

            act.wait_ge(s_te, 1)
            with act.Fori(0, (TILES - 1) // 2) as it:
                for s in range(2):
                    hidden(s, it * 2 + s)
            hidden(0, TILES - 1)

        @block.tensor
        def _(pe):
            pe.wait_ge(s_xn, TT)
            for k in range(KT):
                for i in range(TT):
                    mm = pe.transpose(bank[k][:, i * P:(i + 1) * P], xn[:, i, k * P:(k + 1) * P], ident[:, :])
            mm.then_inc(s_xt, 1)
            pe.wait_ge(s_xts, KT)
            for i in range(TT):
                for k in range(KT):
                    mm = pe.matmul(bank[0][:, i * E:(i + 1) * E], xT[:, k, i * P:(i + 1) * P], rw[:, k, :],
                                   start=(k == 0), stop=(k == KT - 1))
            mm.then_inc(s_lg, 1)
            pe.wait_ge(s_tri, 2)
            pe.wait_ge(s_c, 1)
            for i in range(TT + 1):
                for j in range(min(i, TT)):
                    mm = pe.matmul(bank[1][:, i * E:(i + 1) * E], onesb[:, :], chosenb[:, j, :],
                                   start=(j == 0), stop=(i == TT and j == TT - 1))
                if i < TT:
                    mm = pe.matmul(bank[1][:, i * E:(i + 1) * E], upper[:, :], chosenb[:, i, :], start=(i == 0), stop=True)
            mm.then_inc(s_rk, 1)
            pe.wait_ge(s_xs, 16)
            pe.wait_ge(s_te, 1)
            for n in range((TILES + 1) // 2):
                if n >= 2:
                    pe.wait_ge(s_st_c, n - 1)
                for i in range(min(2, TILES - 2 * n)):
                    for k in range(KT):
                        mm = pe.transpose(bank[n % 2][:, (i * KT + k) * P:(i * KT + k + 1) * P],
                                          xs[:, 2 * n + i, k * P:(k + 1) * P], ident[:, :])
                mm.then_inc(s_st_t, 1)
            pe.wait_ge(s_st_c, (TILES + 1) // 2)

            def hidden(s, tile, uses):
                pe.wait_ge(s_w1[s], 16 * (uses + 1))
                wait_past(pe, s_hr, (tile - 1) * FT)
                for f in range(FT):
                    for k in range(KT):
                        mm = pe.matmul(hp[s][:, f, :], w1[s][:, k, f * P:(f + 1) * P],
                                       xsT[:, bass.ds(tile, 1), k, :].rearrange("p o n -> p (o n)"),
                                       start=(k == 0), stop=(k == KT - 1))
                mm.then_inc(s_h, 1)

            def rows(s, tile):
                e = expert_of(pe, tile)
                if not isinstance(tile, int) or tile >= 2:
                    pe.wait_ge(s_ys, tile - 1)
                for f in range(FT):
                    pe.wait_ge(s_hr, tile * FT + (f + 1))
                    mm = pe.matmul(yp[s][:], hT[s][:, f, :], w2[:, bass.ds(e * FT + f, 1), :].rearrange("p o c -> p (o c)"),
                                   start=(f == 0), stop=(f == FT - 1))
                mm.then_inc(s_y, 1)

            pe.wait_ge(t["s_fw"], 16 * t["n_fw"])
            hidden(0, 0, 0)
            hidden(1, 1, 0)
            rows(0, 0)
            hidden(0, 2, 1)
            rows(1, 1)
            with pe.Fori(1, (TILES - 1) // 2) as it:
                hidden(1, it * 2 + 1, it)
                rows(0, it * 2)
                hidden(0, it * 2 + 2, it + 1)
                rows(1, it * 2 + 1)
            rows(0, TILES - 1)


def build(nc, a, out):
    with ExitStack() as ctx:
        def sb(name, shape, dt=F32):
            return ctx.enter_context(nc.sbuf_tensor(name, shape, dt))

        t = {"x1": sb("x1", [P, TT, C]), "ident": sb("ident", [P, P]), "identb": sb("identb", [P, P], BF16),
             "s_x1": ctx.enter_context(nc.semaphore("x1_ready")),
             "s_x2": ctx.enter_context(nc.semaphore("x2_ready")),
             "s_aw": ctx.enter_context(nc.semaphore("attention_weights_in")),
             "x_in": a["x"], "ctx": a["ctx_1024"]}
        for n in ("q", "k", "v", "o"):
            t["w" + n] = a["L0_xattn_W" + n]
            t["b" + n] = a["L0_xattn_b" + n]
        by_row = "(k p) n -> p k n"
        src = {"wq": a["L0_attn_W_q"].rearrange(by_row, p=P), "wkv": a["L0_attn_W_kv"].rearrange(by_row, p=P),
               "wkr": a["L0_attn_W_krope"].rearrange(by_row, p=P),
               "wqr": a["L0_attn_W_qrope"], "wqd": a["L0_attn_W_qdec"], "wkd": a["L0_attn_W_kdec"],
               "wvd": a["L0_attn_W_vdec"], "g": a["L0_attn_g_kv"].unsqueeze(1), "cos": a["cos"], "sin": a["sin"]}
        t["attn_w"] = {n: sb("a_" + n, s.shape) for n, s in src.items()}
        t["attn_src"] = src
        t["attn_wo"] = a["L0_attn_W_o"]
        cst = sb("cst", [P, sum(n for _, n in TABLES)])
        at = 0
        t["cst"] = {}
        for n, width in TABLES:
            t["cst"][n] = cst[:, at:at + width]
            at += width
        t["rw"], t["rb"] = sb("rw", [P, KT, E]), sb("rb", [P, E])
        t["b1"] = sb("b1", [P, E * FT])
        small = [(cst[:], a["tables"].partition_broadcast(P)), (t["rb"][:], a["L0_ffn_router_b"].partition_broadcast(P)),
                 (t["rw"][:], a["L0_ffn_router_W"].rearrange(by_row, p=P)), (t["b1"][:], a["L0_ffn_b1"])]
        t["ffn_small"] = small
        t["b2_in"], t["w2_in"], t["w1_in"] = a["L0_ffn_b2"], a["L0_ffn_W2"], a["L0_ffn_W1"]
        t["s_fw"] = ctx.enter_context(nc.semaphore("expert_weights_in"))
        t["s_zero"] = ctx.enter_context(nc.semaphore("slots_zeroed"))
        t["n_fw"] = len(small) + 2 * E
        t["slots"] = nc.dram_tensor("slots", [TILES * P, C], F32).ap()
        cross_attention(nc, t, t)
        t["b2"] = sb("b2", [P, E, C])
        t["w2"] = sb("w2", [P, E * FT, C])
        latent_attention(nc, t)
        expert_layer(nc, t, out)


TABLES = (("fall", E), ("fill", TT), ("lower", E * E), ("tile", TILES))


def routing_tables():
    return np.concatenate([np.arange(E, 0, -1), np.arange(TT) * P, np.tril(np.ones((E, E)), -1).ravel(),
                           np.arange(TILES)]).astype(np.float32)


def rope_tables():
    dim = 32
    inv_freq = 1.0 / 10000.0 ** (np.arange(0, dim, 2, dtype=np.float32) / dim)
    freqs = np.outer(np.arange(NQ, dtype=np.float32), inv_freq)
    cos, sin = np.cos(freqs), np.sin(freqs)
    lay = lambda a: np.ascontiguousarray(a.reshape(2, P, dim).transpose(1, 0, 2).astype(np.float32))
    return lay(np.concatenate([cos, cos], -1)), lay(np.concatenate([-sin, sin], -1))


_TRANSPOSED = ("L0_xattn_Wq", "L0_xattn_Wk", "L0_xattn_Wv", "L0_xattn_Wo")
_BY_CHANNEL = ("L0_xattn_bq", "L0_xattn_bk", "L0_xattn_bv")
_BY_GROUP = ("L0_xattn_Wq", "L0_xattn_bq", "L0_xattn_Wk", "L0_xattn_bk")
_INS = ["x", "ctx_1024", "L0_xattn_Wq", "L0_xattn_bq", "L0_xattn_Wk", "L0_xattn_bk", "L0_xattn_Wv", "L0_xattn_bv",
        "L0_xattn_Wo", "L0_xattn_bo", "L0_attn_W_kv", "L0_attn_g_kv", "L0_attn_W_kdec", "L0_attn_W_vdec",
        "L0_attn_W_q", "L0_attn_W_qdec", "L0_attn_W_krope", "L0_attn_W_qrope", "L0_attn_W_o",
        "L0_ffn_router_W", "L0_ffn_router_b", "L0_ffn_W1", "L0_ffn_b1", "L0_ffn_W2", "L0_ffn_b2"]


def kernel(**inputs):
    import concourse.bacc as bacc
    from concourse.bass_utils import run_bass_kernel_spmd as run

    nc = bacc.Bacc("TRN2", target_bir_lowering=False, num_devices=1)
    arrays, aps = {}, {}
    for name in _INS:
        arr = np.asarray(inputs[name])
        if name == "L0_ffn_b1":
            arr = np.ascontiguousarray(arr.reshape(-1, P).T)
        if name in _BY_GROUP:
            arr = arr.reshape(2, GROUPS // 2, HG, D, -1).transpose(1, 0, 3, 2, 4).reshape(arr.shape)
        if name in _BY_CHANNEL:
            arr = arr.reshape(-1, P)
        arr = np.ascontiguousarray(arr.T if name in _TRANSPOSED + _BY_CHANNEL else arr)
        arrays["in_" + name] = arr
        aps[name] = nc.dram_tensor("in_" + name, arr.shape, mybir.dt.from_np(arr.dtype), kind="ExternalInput").ap()
    for name, arr in zip(("cos", "sin", "tables"), (*rope_tables(), routing_tables())):
        arrays["in_" + name] = arr
        aps[name] = nc.dram_tensor("in_" + name, arr.shape, F32, kind="ExternalInput").ap()
    out = nc.dram_tensor("out_0", (B, NQ, C), F32, kind="ExternalOutput").ap()
    build(nc, aps, out)
    r = run(nc, [arrays], core_ids=[0])
    return r.results[0]["out_0"]
```

```python
from contextlib import ExitStack

import numpy as np

import concourse.bass as bass
from concourse import mybir

F32 = mybir.dt.float32
BF16 = mybir.dt.bfloat16
ALU = mybir.AluOpType
ACT = mybir.ActivationFunctionType
AXX = mybir.AxisListType.X

P = 128
B, NQ, C = 2, 256, 256
NKV = 4096
H, D = 16, 16
TOK = B * NQ
TT = TOK // P
KT = C // P
CHUNK = 512
NCHUNK = B * NKV // CHUNK
CT = CHUNK // P
HG = 4
GROUPS = H // HG
NG = B * GROUPS
UNITS = NKV // P
QUARTERS = 4
MAXC = NKV // CHUNK
STACK = 6 * D
LN_EPS = 1e-5
E = 8
F = 1024
FT = F // P
TILES = TOK // P + E - 1


def wait_past(eng, sem, value):
    if not (isinstance(value, int) and value <= 0):
        eng.wait_ge(sem, value)


class Steps:

    def __init__(self, eng, sem):
        self.eng, self.sem, self.n, self.shift = eng, sem, 0, 0

    def mark(self, ins):
        self.n += 1
        ins.then_inc(self.sem, 1)
        return self.n + self.shift

    def link(self, ins):
        self.eng.wait_ge(self.sem, self.mark(ins))


def add_rows(v, dve, t, i, product, written, n):
    v.tensor_tensor(t["x1"][:, i, :], product, t["x1"][:, i, :], ALU.add).then_inc(written, 1)
    dve.wait_ge(written, i + 1)
    v.bn_stats(t["stats"][:, i, :], t["x1"][:, i, :]).then_inc(t["s_ln"], 1)
    dve.wait_ge(t["s_ln"], n + 2 * i + 1)
    v.bn_aggr(t["mv"][:, i, :], t["stats"][:, i, :]).then_inc(t["s_ln"], 1)


def cross_attention(nc, t):
    with ExitStack() as ctx:
        def sb(name, shape, dt=F32):
            return ctx.enter_context(nc.sbuf_tensor(name, shape, dt))

        def ps(name, shape):
            return ctx.enter_context(nc.psum_tensor(name, shape, F32))

        def sem(name):
            return ctx.enter_context(nc.semaphore(name))

        x1, ident, identb = t["x1"], t["ident"], t["identb"]

        k_parts = nc.dram_tensor("k_parts", [NG, 3 * D, HG, NKV], BF16).ap()
        q_stack = nc.dram_tensor("q_stack", [NG, STACK, HG, NQ], BF16).ap()
        Q_ROWS = (0, 0, 0, 1, 1, 2)
        v_rows = nc.dram_tensor("v_rows", [NG, P, UNITS, HG, D + 1], F32).ap()

        wq = sb("wq", [P, KT, C])
        wk = sb("wk", [P, KT, C])
        wv = sb("wv", [P, KT, C])
        wo = sb("wo", [P, KT, C])
        bq = sb("bq", [P, KT])
        bk = sb("bk", [P, KT])
        bv = sb("bv", [P, KT])
        bo = sb("bo", [P, C])
        x = sb("x", [P, TT, C])
        xn = sb("xn", [P, TT, C])
        xT = sb("xT", [P, KT, TOK])
        stats, mv = t["stats"], t["mv"]
        sd = sb("sd", [P, TT, 2])
        ctx_in = [sb(f"ctx_in{i}", [P, CT, C]) for i in range(2)]
        ctxT = [sb(f"ctxT{i}", [P, KT, CHUNK]) for i in range(2)]
        kf = sb("kf", [P, KT, CHUNK])
        rest = sb("rest", [P, KT, CHUNK])
        parts = [sb(f"parts{i}", [P, KT, 3, CHUNK], BF16) for i in range(2)]
        q3 = sb("q3", [P, KT, 3, TOK], BF16)
        v_out = [sb(f"v_out{i}", [P, GROUPS, CT, HG, D + 1]) for i in range(2)]
        kst = [sb(f"kst{i}", [STACK + 2, HG, NKV], BF16) for i in range(2)]
        qst = [sb(f"qst{i}", [STACK + 2, HG, NQ], BF16) for i in range(2)]
        vg = [sb(f"vg{i}", [P, UNITS, HG, D + 1]) for i in range(2)]
        probs = [sb(f"probs{i}", [P, HG, NQ]) for i in range(4)]
        maxes = sb("maxes", [P, HG * 2, MAXC])
        mrow = sb("mrow", [P, HG * 2])
        shift = sb("shift", [P, HG * 2, 2], BF16)
        acc_s = sb("acc_s", [P, NQ])
        recip = sb("recip", [P, 2, HG])
        o = sb("o", [P, 2, NG, HG, D])
        oT = sb("oT", [P, KT, TOK])

        banks = [ps(f"bank{i}", [P, 512]) for i in range(4)]
        score_a = ps("score_a", [P, HG, NQ])
        score_b = ps("score_b", [P, HG, NQ])

        side = [bank[:, :] for bank in banks[0:3]]
        acc = banks[3][:, 0:NQ]
        out_rows = [score[:, 2 * k, :] for score in (score_a, score_b) for k in range(2)]
        q_banks = [score_b[:, 2 * k:2 * k + 2, :].rearrange("p a n -> p (a n)") for k in range(KT)]
        scores = [score_a[:, :, :].rearrange("p h n -> p (h n)"), score_b[:, :, :].rearrange("p h n -> p (h n)")]

        s_x = sem("x_in")
        s_kw = sem("key_weights_in")
        s_vw = sem("value_weights_in")
        s_w = sem("other_weights_in")
        s_ctx = [sem(f"ctx_in_{i}") for i in range(2)]
        s_id = sem("ident_ready")
        s_ones = sem("ones_ready")
        s_v = sem("vector_steps")
        s_var = sem("variance_ready")
        s_qf = sem("query_product_copied")
        s_sd = sem("deviation_ready")
        s_xn = sem("normed_ready")
        s_xt = sem("x_transposed")
        s_xts = sem("x_transposed_copied")
        s_qp = sem("query_product")
        s_qs = sem("query_parts_ready")
        s_qst = sem("query_parts_stored")
        s_tp = sem("ctx_transposed")
        s_tc = sem("ctx_transposed_copied")
        s_kp = sem("key_product")
        s_kf = sem("keys_copied")
        s_kh = sem("key_high_ready")
        s_kr = sem("key_parts_ready")
        s_vp = sem("value_product")
        s_vr = sem("values_ready")
        s_ks = [sem(f"key_parts_stored_{i}") for i in range(2)]
        s_vs = [sem(f"values_stored_{i}") for i in range(2)]
        s_kq = [[sem(f"key_stack_in_{i}_{q}") for q in range(QUARTERS)] for i in range(2)]
        s_q = [sem(f"query_stack_in_{i}") for i in range(2)]
        s_vg = [sem(f"group_values_in_{i}") for i in range(2)]
        s_kq_first = [[sem(f"first_key_stack_in_{i}_{q}") for q in range(QUARTERS)] for i in range(2)]
        s_q_first = [sem(f"first_query_stack_in_{i}") for i in range(2)]
        s_vg_first = sem("first_group_values_in")
        s_sc = sem("scores_ready")
        s_ex = sem("probs_ready")
        s_pf = sem("probs_free")
        s_af = sem("acc_free")
        s_job = sem("side_bank_written")
        s_jd = sem("side_bank_read")
        s_sh = sem("shift_ready")
        s_ot = sem("out_transposed")
        s_otc = sem("out_transposed_copied")
        s_y = sem("out_product")

        LOADS = 5

        HEAD_PAIR = 4
        head_banks = [score_b[:, 0:2, :].rearrange("p a n -> p (a n)"), score_b[:, 2:4, :].rearrange("p a n -> p (a n)")]

        def head_range(n):
            chunks, jobs = NCHUNK - 1 - 2 * HEAD_PAIR, HG * 2 * MAXC
            a = n - 2 * HEAD_PAIR
            if n == NCHUNK - 1:
                return jobs, jobs
            return jobs * a // chunks, jobs * (a + 1) // chunks

        def free_job(p, base):
            return base + (p - 2 if p >= 3 else {0: -1, 1: 0, 2: -2}[p])

        HEAD_JOBS = HG * 2 * MAXC + 2
        BODY_JOBS = HEAD_JOBS + 1
        FIRST_T, LAST_T = 1, 26

        def max_jobs_at(tile):
            n, span = HG * 2 * MAXC, LAST_T - FIRST_T + 1
            a = n * max(0, min(span, tile - FIRST_T)) // span
            b = n * max(0, min(span, tile - FIRST_T + 1)) // span
            return range(a, b)

        HALF = NKV // CHUNK
        R = HG * D

        def load_queries(eng, s, i, done):
            eng.dma_start(qst[s][0:STACK, :, :].rearrange("p j n -> p (j n)"),
                         q_stack[bass.ds(i, 1), :, :, :].rearrange("o p j n -> p (o j n)")).then_inc(done, 16)

        def load_keys(eng, s, i, q, done):
            n = NKV // QUARTERS
            row = 0
            for part_rows in (3 * D, 2 * D, D):
                src = k_parts[bass.ds(i, 1), 0:part_rows, :, q * n:(q + 1) * n].rearrange("o p j n -> p (o j) n")
                eng.dma_start(kst[s][row:row + part_rows, :, q * n:(q + 1) * n], src).then_inc(done, 16)
                row += part_rows

        def load_values(eng, s, i, done):
            src = v_rows[bass.ds(i, 1), :, :, :, :].rearrange("o p u h e -> p (o u h e)")
            eng.dma_start(vg[s][:].rearrange("p u h e -> p (u h e)"), src).then_inc(done, 16)

        block = ctx.enter_context(nc.Block())

        @block.gpsimd
        def _(eng):
            eng.memset(ident[:, :], 0.0).then_inc(s_pf, len(probs))
            eng.memset(identb[:, :], 0.0).then_inc(s_id, 1)
            eng.wait_ge(s_pf, len(probs))
            eng.wait_ge(s_id, 1)
            for m in (ident, identb):
                eng.affine_select(out=m[:, :], in_=m[:, :], compare_op=ALU.not_equal, fill=1.0,
                                  base=0, pattern=[[-1, P]], channel_multiplier=1).then_inc(s_id, 1)
            eng.wait_ge(s_id, 3)
            for n, v in enumerate(v_out):
                eng.memset(v[:], 1.0).then_inc(s_ones, 1)
                eng.wait_ge(s_ones, n + 1)
            for n, k in enumerate(kst):
                eng.memset(k[STACK:STACK + 2, :, :], 1.0).then_inc(s_ones, 1)
                eng.wait_ge(s_ones, n + 3)
            eng.wait_ge(s_qs, 1)
            for copy, part in enumerate(Q_ROWS):
                for g in range(2):
                    for b in range(B):
                        i = b * GROUPS + g * KT
                        dst = q_stack[i:i + KT, copy * D:(copy + 1) * D, :, :]
                        eng.dma_start(dst.rearrange("k d j n -> (d j) k n"),
                                     q3[g * R:(g + 1) * R, :, part, b * NQ:(b + 1) * NQ]).then_inc(s_qst, 16)

            eng.wait_ge(s_qst, 16 * 2 * B * len(Q_ROWS))
            load_queries(eng, 0, 0, s_q_first[0])
            load_queries(eng, 1, 1, s_q_first[1])
            for q in range(QUARTERS):
                for s in range(2):
                    eng.wait_ge(s_ks[s], 2 * 16 * (HALF // (2 * QUARTERS)) * (q + 1))
                load_keys(eng, 0, 0, q, s_kq_first[0][q])
            for s in range(2):
                eng.wait_ge(s_vs[s], 16 * (HALF // 2))
            eng.wait_ge(s_tp, HALF + 3)
            load_values(eng, 0, 0, s_vg_first)
            for q in range(QUARTERS):
                eng.wait_ge(s_tp, HALF + 4 + q)
                load_keys(eng, 1, 1, q, s_kq_first[1][q])

        @block.sync
        def _(sp):
            def weights(dst, src, done):
                sp.dma_start(dst[:], src.rearrange("(k p) n -> p k n", p=P)).then_inc(done, 16)

            ctx_rows = t["ctx"].rearrange("b (n p j) c -> p (b n) j c", p=P, j=CT)

            def first_chunk(s):
                sp.dma_start(ctx_in[s][:], ctx_rows[:, s, :, :]).then_inc(s_ctx[s], 16)

            sp.dma_start(x[:], t["x_in"].rearrange("b (q p) c -> p (b q) c", p=P)).then_inc(s_x, 16)
            first_chunk(0)
            weights(wk, t["wk"], s_kw)
            sp.dma_start(bk[:], t["bk"]).then_inc(s_kw, 16)
            first_chunk(1)
            weights(wv, t["wv"], s_vw)
            weights(wq, t["wq"], s_w)
            for dst, src in ((bq, t["bq"]), (bv, t["bv"])):
                sp.dma_start(dst[:], src).then_inc(s_w, 16)
            sp.dma_start(bo[:], t["bo"].partition_broadcast(P)).then_inc(s_w, 16)
            weights(wo, t["wo"], s_w)
            def store(s, n, b, cn):
                sp.wait_ge(s_kr, n + 1)
                for g in range(2):
                    i = b * GROUPS + g * KT
                    dst = k_parts[i:i + KT, :, :, bass.ds(cn * CHUNK, CHUNK)]
                    sp.dma_start(dst.rearrange("k (a d) j n -> (d j) (k a) n", d=D),
                                 parts[s][g * R:(g + 1) * R, :, :, :].rearrange("p k a n -> p (k a) n")).then_inc(s_ks[s], 16)
                sp.wait_ge(s_vr, n + 1)
                dst = v_rows[b * GROUPS:(b + 1) * GROUPS, :, bass.ds(cn * CT, CT), :, :]
                sp.dma_start(dst.rearrange("g p j h e -> p g (j h e)"),
                             v_out[s][:].rearrange("p g j h e -> p g (j h e)")).then_inc(s_vs[s], 16)

            def project(it, b, more):
                for s in range(2):
                    cn = it * 2 + s
                    n = cn + b * HALF
                    if more:
                        sp.wait_ge(s_tp, n + 1)
                        sp.dma_start(ctx_in[s][:], ctx_rows[:, bass.ds(n + 2, 1), :, :].rearrange("p o j c -> p (o j) c")).then_inc(s_ctx[s], 16)
                    if not (isinstance(cn, int) and cn == 0):
                        store(1 - s, n - 1, b, cn - 1)
                    elif b > 0:
                        store(1 - s, n - 1, b - 1, HALF - 1)

            for b in range(B):
                project(0, b, True)
                with sp.Fori(1, HALF // 2 - b) as it:
                    project(it, b, True)
            project(HALF // 2 - 1, B - 1, False)
            store(1, NCHUNK - 1, B - 1, HALF - 1)
            load_values(sp, 1, 1, s_vg[1])
            for n, src in t["attn_src"].items():
                sp.dma_start(t["attn_w"][n][:], src).then_inc(t["s_aw"], 16)
            for s in range(2):
                sp.wait_ge(s_ks[s], 2 * 16 * (NCHUNK // 2))
                sp.wait_ge(s_vs[s], 16 * (NCHUNK // 2))

            def next_group(s, i):
                for q in range(QUARTERS):
                    if q == QUARTERS - 1:
                        sp.wait_ge(s_sc, (i - 1) * UNITS)
                        load_queries(sp, s, i, s_q[s])
                    sp.wait_ge(s_pf, (i - 2) * UNITS + (len(probs) + (UNITS // QUARTERS) * (q + 1)))
                    load_keys(sp, s, i, q, s_kq[s][q])
                load_values(sp, s, i, s_vg[s])

            with sp.Fori(1, NG // 2) as it:
                for s in range(2):
                    next_group(s, it * 2 + s)
            sp.wait_ge(t["s_aw"], 16 * len(t["attn_src"]))

        @block.scalar
        def _(act):
            act.wait_ge(s_var, 1)
            act.activation(sd[:, :, 1], sd[:, :, 0], ACT.Sqrt).then_inc(s_sd, 1)

            def copy_transposed(n, s):
                act.wait_ge(s_tp, n + 1)
                act.activation(ctxT[s][:, 0, :], banks[0][:, :], ACT.Copy).then_inc(s_tc, 1)

            def project(it, more):
                for s in range(2):
                    n = it * 2 + s
                    if more or s == 0:
                        copy_transposed(n + 1, 1 - s)
                    wait_past(act, s_kr, n)
                    for k in range(KT):
                        act.wait_ge(s_kp, n * KT + (k + 1))
                        act.activation(kf[:, k, :], banks[2 + k][:, :], ACT.Identity, bias=bk[:, k:k + 1]).then_inc(s_kf, 1)
                    act.wait_ge(s_kf, n * KT + KT)
                    wait_past(act, s_ks[s], it * 32)
                    act.activation(parts[s][:, :, 0, :], kf[:, :, :], ACT.Copy).then_inc(s_kh, 1)
                    act.wait_ge(s_vp, n + 1)
                    wait_past(act, s_vs[s], it * 16)
                    for g in range(GROUPS):
                        ins = act.activation(v_out[s][:, g, :, :, 0:D],
                                             score_a[:, :, g * HG * D:(g + 1) * HG * D].rearrange("p t (j d) -> p t j d", d=D),
                                             ACT.Copy)
                    ins.then_inc(s_vr, 1)

            act.wait_ge(s_kw, 32)
            act.wait_ge(s_ones, 2)
            copy_transposed(0, 0)
            project(0, True)
            with act.Fori(1, NCHUNK // 2 - 1) as it:
                project(it, True)
            project(NCHUNK // 2 - 1, False)

            def copy_output(i):
                act.wait_ge(s_pf, (i + 1) * UNITS + len(probs))
                act.activation(acc_s[:], acc, ACT.Copy).then_inc(s_af, 1)

            def probabilities(i, first):
                for u in range(UNITS):
                    n = i * UNITS + u
                    r = u % len(probs)
                    act.wait_ge(s_sc, n + 1)
                    act.wait_ge(s_pf, n + 1)
                    act.activation(probs[r][:].rearrange("p h n -> p (h n)"),
                                   scores[u % 2], ACT.Exp).then_inc(s_ex, 1)
                    if u == 0 and not first:
                        copy_output(i - 1)

            probabilities(0, True)
            with act.Fori(0, (NG - 2) // 2) as it:
                probabilities(it * 2 + 1, False)
                probabilities(it * 2 + 2, False)
            probabilities(NG - 1, False)
            copy_output(NG - 1)
            act.activation(sd[:, :, 1], sd[:, :, 1], ACT.Sqrt)

        @block.vector
        def _(dve):
            st = Steps(dve, s_v)
            v = nc.vector
            dve.wait_ge(s_x, 16)
            for i in range(TT):
                v.bn_stats(stats[:, i, :], x[:, i, :]).then_inc(s_v, 1)
            st.n = TT
            dve.wait_ge(s_v, TT)
            for i in range(TT):
                last = st.mark(v.bn_aggr(mv[:, i, :], stats[:, i, :]))
            dve.wait_ge(s_v, last)
            v.tensor_scalar(sd[:, :, 0], mv[:, :, 1], LN_EPS, None, ALU.add).then_inc(s_var, 1)
            dve.wait_ge(s_sd, 1)
            st.link(v.reciprocal(sd[:, :, 0], sd[:, :, 1]))
            for i in range(TT):
                v.tensor_scalar(xn[:, i, :], x[:, i, :], mv[:, i, 0:1], sd[:, i, 0:1],
                                ALU.subtract, ALU.mult).then_inc(s_xn, 1)
            def split(src, dst, mid_sem, high):
                if high:
                    st.link(v.tensor_copy(dst[:, :, 0, :], src))
                st.link(v.tensor_tensor(rest[:], src, dst[:, :, 0, :], ALU.subtract))
                st.link(v.tensor_copy(dst[:, :, 1, :], rest[:]))
                v.tensor_tensor(dst[:, :, 2, :], rest[:], dst[:, :, 1, :], ALU.subtract).then_inc(mid_sem, 1)

            def copy_transposed(n, s):
                dve.wait_ge(s_tp, n + 1)
                v.tensor_copy(ctxT[s][:, 1, :], banks[1][:, :]).then_inc(s_tc, 1)

            def max_job(job, slot, k, c):
                dve.wait_ge(s_job, job + 1)
                v.reduce_max(maxes[:, k, c:c + 1], slot[:, :], AXX).then_inc(s_jd, 1)

            def make_shift(job):
                dve.wait_ge(s_jd, job)
                st.link(v.reduce_max(mrow[:], maxes[:], AXX))
                st.link(v.tensor_scalar(shift[:, :, 0], mrow[:], -1.0, None, ALU.mult))
                v.scalar_tensor_tensor(out=shift[:, :, 1], in0=mrow[:], scalar=-1.0, in1=shift[:, :, 0],
                                       op0=ALU.mult, op1=ALU.subtract).then_inc(s_sh, 1)

            def shift_job(job, slot, s, a):
                dve.wait_ge(s_job, job + 1)
                v.tensor_copy(qst[s][STACK:STACK + 2, 2 * a:2 * a + 2, :].rearrange("p h n -> p (h n)"),
                              slot[STACK:STACK + 2, :]).then_inc(s_jd, 1)

            def out_job(job, slot, i):
                dve.wait_ge(s_job, job + 1)
                dve.wait_ge(s_jd, job)
                rows = slot[:, 0:2 * P].rearrange("p (q j r) -> p q j r", q=2, j=HG)
                st.link(v.reciprocal(recip[:], rows[:, :, :, D]))
                v.tensor_tensor(o[:, :, bass.ds(i, 1), :, :].rearrange("p q o j d -> p q (o j) d"),
                                rows[:, :, :, 0:D], recip[:].unsqueeze(3).to_broadcast([P, 2, HG, D]),
                                ALU.mult).then_inc(s_jd, 1)

            PER_PAIR = 4

            def project(it, more, head=None):
                for s in range(2):
                    n = it * 2 + s
                    if more or s == 0:
                        copy_transposed(n + 1, 1 - s)
                    if head:
                        head(n, 0)
                    dve.wait_ge(s_kh, n + 1)
                    wait_past(dve, s_ks[s], it * 32)
                    st.link(v.tensor_tensor(rest[:], kf[:], parts[s][:, :, 0, :], ALU.subtract))
                    if head:
                        head(n, 1)
                    st.link(v.tensor_copy(parts[s][:, :, 1, :], rest[:]))
                    if head:
                        head(n, 2)
                    v.tensor_tensor(parts[s][:, :, 2, :], rest[:], parts[s][:, :, 1, :], ALU.subtract).then_inc(s_kr, 1)
                    if head:
                        head(n, 3)

            def head_jobs(n, step):
                if n == NCHUNK - 1:
                    if step == 0:
                        make_shift(HEAD_JOBS - 2)
                    if step == 1:
                        for a in range(2):
                            shift_job(HEAD_JOBS - 2 + a, head_banks[a], 0, a)
                    return
                a, b = head_range(n)
                lots = [a, min(a + 5, b), min(a + 7, b), min(a + 9, b), b]
                for m in range(lots[step], lots[step + 1]):
                    max_job(m, head_banks[m % 2], m % 8, m // 8)

            copy_transposed(0, 0)
            dve.wait_ge(s_xt, 1)
            for k in range(KT):
                v.tensor_copy(xT[:, k, :], q_banks[k]).then_inc(s_xts, 1)
            project(0, True)
            qf = xn[:].rearrange("p a c -> p (a c)").rearrange("p (k n) -> p k n", k=KT)
            dve.wait_ge(s_qp, 1)
            dve.wait_ge(s_w, LOADS * 16)
            for k in range(KT):
                v.tensor_scalar(qf[:, k, :], q_banks[k], bq[:, k:k + 1], D ** -0.5,
                                ALU.add, ALU.mult).then_inc(s_qf, 1)
            dve.wait_ge(s_qf, KT)
            dve.wait_ge(s_kr, 2)
            split(qf, q3, s_qs, True)
            dve.wait_ge(s_qs, 1)
            for i in range(TT):
                v.tensor_tensor(x1[:, i, :], x[:, i, :], bo[:, :], ALU.add)
            with dve.Fori(1, HEAD_PAIR) as it:
                st.shift = (it - 1) * PER_PAIR
                n0 = st.n
                project(it, True)
                assert st.n - n0 == PER_PAIR
            st.shift = (HEAD_PAIR - 2) * PER_PAIR
            for it in range(HEAD_PAIR, NCHUNK // 2):
                project(it, it < NCHUNK // 2 - 1, head_jobs)

            PER_LOOP = 6
            def group(slot_of, base, i, s, first, last):
                p = 0
                if not first:
                    out_job(base, slot_of(0), i - 1)
                    p = 1
                if last:
                    return
                for m in range(HEAD_JOBS - 2):
                    max_job(base + p, slot_of(p), m % 8, m // 8)
                    p += 1
                make_shift(base + p)
                for a in range(2):
                    shift_job(base + p, slot_of(p), 1 - s, a)
                    p += 1

            base = HEAD_JOBS
            group(lambda p: side[(p + 2) % 3], base, 0, 0, True, False)
            base = 2 * HEAD_JOBS
            n0 = st.n
            n_shift = st.shift
            with dve.Fori(0, (NG - 2) // 2) as it:
                st.shift = it * PER_LOOP + n_shift
                group(lambda p: side[p % 3], it * (2 * BODY_JOBS) + base, it * 2 + 1, 1, False, False)
                group(lambda p: side[(BODY_JOBS + p) % 3], it * (2 * BODY_JOBS) + (base + BODY_JOBS), it * 2 + 2, 0, False, False)
                assert st.n - n0 == PER_LOOP, st.n - n0
            st.shift = n_shift + ((NG - 2) // 2 - 1) * PER_LOOP
            base = 2 * HEAD_JOBS + (NG - 2) * BODY_JOBS
            group(lambda p: side[p % 3], base, NG - 1, 1, False, True)
            out_job(base + 1, side[1], NG - 1)

            dve.wait_ge(s_ot, 1)
            for k in range(KT):
                v.tensor_scalar(oT[:, k, :], banks[k][:, :], bv[:, k:k + 1], None, ALU.add).then_inc(s_otc, 1)
            for i in range(TT):
                dve.wait_ge(s_y, i + 1)
                add_rows(v, dve, t, i, out_rows[i], t["s_x1"], 0)

        @block.tensor
        def _(pe):
            def transposes(n, s, uses):
                pe.wait_ge(s_ctx[s], 16 * (uses + 1))
                wait_past(pe, s_tc, n * KT)
                for k in range(KT):
                    for j in range(CT):
                        mm = pe.transpose(banks[k][:, j * P:(j + 1) * P], ctx_in[s][:, j, k * P:(k + 1) * P], ident[:, :])
                mm.then_inc(s_tp, 1)

            def max_job(free, bank, s, m):
                k, c = m % 8, m // 8
                if free is not None:
                    pe.wait_ge(s_jd, free)
                pe.matmul(bank, qst[s][0:STACK, k // 2, (k % 2) * P:(k % 2 + 1) * P],
                          kst[s][0:STACK, k // 2, c * CHUNK:(c + 1) * CHUNK], start=True, stop=True).then_inc(s_job, 1)

            def shift_job(free, slot, a):
                pe.wait_ge(s_jd, free)
                for m in range(4):
                    mm = pe.matmul(slot[STACK:STACK + 2, m * P:(m + 1) * P], shift[:, 4 * a + m, :],
                                   identb[:, :], start=True, stop=True)
                mm.then_inc(s_job, 1)

            def project(it, more, head=False):
                for s in range(2):
                    n = it * 2 + s
                    todo = list(range(*head_range(n))) if head else []

                    def head_job():
                        if todo:
                            m = todo.pop(0)
                            if m == 0:
                                pe.wait_ge(s_q_first[0], 16)
                            if m % 16 == 0:
                                pe.wait_ge(s_kq_first[0][m // 16], 48)
                            max_job(m - 1 if m >= 2 else None, head_banks[m % 2], 0, m)

                    if more or s == 0:
                        transposes(n + 1, 1 - s, it + s)
                    pe.wait_ge(s_tc, n * KT + KT)
                    wait_past(pe, s_kf, n * KT)
                    for h in range(KT):
                        for k in range(KT):
                            mm = pe.matmul(banks[2 + h][:, :], wk[:, k, h * P:(h + 1) * P], ctxT[s][:, k, :],
                                           start=(k == 0), stop=(k == KT - 1))
                            if k == KT - 1:
                                mm.then_inc(s_kp, 1)
                            head_job()
                    if isinstance(n, int) and n == NCHUNK - 1:
                        pe.wait_ge(s_sh, 1)
                        for a in range(2):
                            shift_job(HEAD_JOBS - 2, head_banks[a], a)
                    wait_past(pe, s_vr, n)
                    for j in range(CT):
                        for k in range(KT):
                            mm = pe.matmul(score_a[:, j, :], ctxT[s][:, k, j * P:(j + 1) * P], wv[:, k, :],
                                           start=(k == 0), stop=(k == KT - 1))
                            if j == CT - 1 and k == KT - 1:
                                mm.then_inc(s_vp, 1)
                            head_job()
                    assert not todo

            pe.wait_ge(s_id, 3)
            transposes(0, 0, 0)
            pe.wait_ge(s_xn, TT)
            for k in range(KT):
                for i in range(TT):
                    mm = pe.transpose(q_banks[k][:, i * P:(i + 1) * P], xn[:, i, k * P:(k + 1) * P], ident[:, :])
            mm.then_inc(s_xt, 1)
            pe.wait_ge(s_kw, 32)
            pe.wait_ge(s_vw, 16)
            project(0, True)
            pe.wait_ge(s_xts, KT)
            pe.wait_ge(s_w, LOADS * 16)
            for h in range(KT):
                for k in range(KT):
                    mm = pe.matmul(q_banks[h], wq[:, k, h * P:(h + 1) * P], xT[:, k, :],
                                   start=(k == 0), stop=(k == KT - 1))
            mm.then_inc(s_qp, 1)
            with pe.Fori(1, HEAD_PAIR) as it:
                project(it, True)
            for it in range(HEAD_PAIR, NCHUNK // 2):
                project(it, it < NCHUNK // 2 - 1, True)

            def out_job(free, slot, copied):
                pe.wait_ge(s_jd, free)
                pe.wait_ge(s_af, copied)
                for q in range(2):
                    mm = pe.transpose(slot[:, q * P:(q + 1) * P], acc_s[:, q * P:(q + 1) * P], ident[:, :])
                mm.then_inc(s_job, 1)

            def unit_scores(s, n, u):
                if n is not None:
                    pe.wait_ge(s_ex, n - 1)
                for j in range(HG):
                    mm = pe.matmul((score_a, score_b)[u % 2][:, j, :], kst[s][:, j, u * P:(u + 1) * P],
                                   qst[s][:, j, :], start=True, stop=True)
                mm.then_inc(s_sc, 1)

            def unit_values(s, n, u):
                pe.wait_ge(s_ex, n + 1)
                for j in range(HG):
                    mm = pe.matmul(acc[32 * j:32 * j + D + 1, :], vg[s][:, u, j, :], probs[u % len(probs)][:, j, :],
                                   start=(u == 0), stop=(u == UNITS - 1))
                mm.then_inc(s_pf, 1)

            def group(slot_of, base, free, i, s, uses, first, last):
                p = 0
                for u in range(UNITS):
                    n = i * UNITS + u
                    if u + 2 < UNITS:
                        unit_scores(s, n + 2 if not first or u > 0 else n + 2, u + 2)
                    elif not last:
                        if u + 2 == UNITS:
                            pe.wait_ge(s_jd, base + p)
                        unit_scores(1 - s, n + 2, u + 2 - UNITS)
                    if u == 0:
                        if first:
                            pe.wait_ge(s_vg_first, 16)
                        else:
                            pe.wait_ge(s_vg[s], 16 * (uses + s))
                        pe.wait_ge(s_af, i)
                    unit_values(s, n, u)
                    if u == 1 and not first:
                        out_job(free(0), slot_of(0), i)
                        p = 1
                    if last:
                        continue
                    for m in max_jobs_at(u):
                        nxt = uses + (1 if s == 1 else 0)
                        if m == 0:
                            pe.wait_ge(s_q_first[1] if first else s_q[1 - s], 16 if first else 16 * nxt)
                        if m % 16 == 0:
                            pe.wait_ge((s_kq_first[1] if first else s_kq[1 - s])[m // 16], 48 if first else 48 * nxt)
                        max_job(free(p), slot_of(p), 1 - s, m)
                        p += 1
                    if u == LAST_T + 3:
                        pe.wait_ge(s_sh, i + 2)
                        for a in range(2):
                            shift_job(free(p), slot_of(p), a)
                            p += 1

            pe.wait_ge(s_jd, HEAD_JOBS)
            pe.wait_ge(s_ones, 4)
            pe.wait_ge(s_kf, NCHUNK * KT)
            pe.wait_ge(s_vr, NCHUNK)
            for u in range(2):
                unit_scores(0, None, u)
            group(lambda p: side[(p + 2) % 3], HEAD_JOBS, lambda p: HEAD_JOBS + p - 2, 0, 0, 0, True, False)
            with pe.Fori(0, (NG - 2) // 2) as it:
                base = it * (2 * BODY_JOBS) + 2 * HEAD_JOBS
                group(lambda p: side[p % 3], base, lambda p: free_job(p, base), it * 2 + 1, 1, it, False, False)
                group(lambda p: side[(BODY_JOBS + p) % 3], base + BODY_JOBS, lambda p: base + (BODY_JOBS + p - 2),
                      it * 2 + 2, 0, it + 1, False, False)
            base = 2 * HEAD_JOBS + (NG - 2) * BODY_JOBS
            group(lambda p: side[p % 3], base, lambda p: free_job(p, base), NG - 1, 1, (NG - 2) // 2, False, True)
            out_job(base, side[1], NG)

            pe.wait_ge(s_jd, base + 2)
            for k in range(KT):
                for i in range(TT):
                    b, q = i // 2, i % 2
                    rows = o[:, q, b * GROUPS + 2 * k:b * GROUPS + 2 * k + 2, :, :].rearrange("p g j d -> p (g j d)")
                    mm = pe.transpose(banks[k][:, i * P:(i + 1) * P], rows, ident[:, :])
            mm.then_inc(s_ot, 1)
            pe.wait_ge(s_otc, KT)
            for i in range(TT):
                for k in range(KT):
                    mm = pe.matmul(out_rows[i], oT[:, k, i * P:(i + 1) * P], wo[:, k, :],
                                   start=(k == 0), stop=(k == KT - 1))
                mm.then_inc(s_y, 1)


def latent_attention(nc, t):
    T = NQ
    RQ, RK, RD = 128, 64, 32
    HS = 64
    HD = RD + D
    HV = P // HG
    PAIRS = H // 2
    SCALE = float(1.0 / np.sqrt(np.float32(HD)))
    with ExitStack() as ctx:
        def sb(name, shape, dt=F32):
            return ctx.enter_context(nc.sbuf_tensor(name, shape, dt))

        def sem(name):
            return ctx.enter_context(nc.semaphore(name))

        units = [(b, q, g) for b in range(B) for g in range(H // HG) for q in range(2)]
        x1, ident, identb = t["x1"], t["ident"], t["identb"]
        w = t["attn_w"]
        stats, mv = t["stats"], t["mv"]
        sd = sb("a_sd", [P, TT, 2])
        xn = sb("a_xn", [P, TT, C])
        xT = sb("a_xT", [P, KT, TOK])
        qcT = sb("qcT", [RQ, TOK])
        kv = sb("kv", [P, TT, RK])
        kv2 = sb("kv2", [P, TT, RK])
        ms = sb("ms", [P, TT])
        rms = sb("rms", [P, TT])
        kvT = sb("kvT", [RK, TOK])
        rot = [sb(f"rot{i}", [P, 2, H, RD]) for i in range(2)]
        q_rows = sb("q_rows", [P, TT, H, HS])
        k_rows = sb("k_rows", [P, TT, H, HS])
        v_rows = sb("va_rows", [P, TT, H, HV])
        wo = sb("a_wo", [P, H // HG, C])
        qT = sb("qT", [P, PAIRS, TOK])
        kT = sb("kT", [P, PAIRS, TOK])
        diag = sb("diag", [P, P], BF16)
        zeros = sb("zeros", [P, C])
        pr = [sb(f"pr{i}", [P, HG, T]) for i in range(2)]
        prT = [sb(f"prT{i}", [P, HG, 2, P]) for i in range(2)]
        top = sb("a_top", [P, 2, HG])
        ntop = sb("a_ntop", [P, 2, HG])
        rtot = sb("a_rtot", [P, T])
        pick = sb("pick", [P, HG, HV])
        oT = q_rows[:, 0:2, :, :].rearrange("p a h d -> p (a h d)").rearrange("p (g n) -> p g n", g=H // HG)
        pairs = [ctx.enter_context(nc.psum_tensor(f"a_bank{i}", [P, 2, 512], F32)) for i in range(4)]
        vbank = [pairs[i // 2][:, i % 2, :] for i in range(4)]
        abank = [pairs[2 + i // 2][:, i % 2, :] for i in range(4)]

        s_st = sem("a_steps")
        s_var = sem("a_variance_ready")
        s_sd = sem("a_deviation_ready")
        s_xn = sem("a_normed_ready")
        s_vw = sem("a_vector_bank_written")
        s_vr = sem("a_vector_bank_read")
        s_aw = sem("a_scalar_bank_written")
        s_ar = sem("a_scalar_bank_read")
        s_ms = sem("a_mean_square_ready")
        s_rms = sem("a_rms_ready")
        s_kvn = sem("a_latent_normed")
        s_pad = sem("a_padding_ready")
        s_rm = sem("a_rotary_products_ready")
        s_qr = sem("a_query_rotated")
        s_qr2 = sem("a_query_content_copied")
        s_kr = sem("a_key_rotated")
        s_s = sem("a_scores_ready")
        s_nt = sem("a_maxima_ready")
        s_p = sem("a_probs_ready")
        s_t = sem("a_probs_transposed")
        s_tc = sem("a_probs_transposed_copied")
        s_ps = sem("a_sums_spread")
        s_on = sem("a_output_normed")
        s_o = sem("a_output_ready")
        s_oc = sem("a_output_copied")
        s_wo = sem("a_out_weights_in")
        s_y = sem("a_out_product")

        NU = len(units)
        ROTARY_JOBS = (4, 5, 6, 8, 9, 10, 11, 12)
        block = ctx.enter_context(nc.Block())

        @block.sync
        def _(sp):
            for dst, src in t["ffn_small"]:
                sp.dma_start(dst, src).then_inc(t["s_fw"], 16)
            for e in range(E):
                sp.dma_start(t["b2"][:, e, :], t["b2_in"][e, :].partition_broadcast(P)).then_inc(t["s_fw"], 16)
                sp.dma_start(t["w2"][:, e * FT:(e + 1) * FT, :], t["w2_in"][e, :, :].rearrange("(f p) c -> p f c", p=P)).then_inc(t["s_fw"], 16)
            sp.wait_ge(s_pad, 9)
            for j in range(HG):
                sp.dma_start(wo[j * HV:j * HV + D, :, :], t["attn_wo"].rearrange("(g j d) c -> j d g c", j=HG, d=D)[j, :, :, :]).then_inc(s_wo, 16)
            sp.dma_start(t["slots"].rearrange("(t p) c -> p t c", p=P),
                         zeros[:].unsqueeze(1).to_broadcast([P, TILES, C])).then_inc(t["s_zero"], 16)
            sp.wait_ge(t["s_fw"], 16 * t["n_fw"])
            sp.wait_ge(t["s_zero"], 16)
            sp.wait_ge(s_wo, HG * 16)

        @block.gpsimd
        def _(eng):
            eng.memset(q_rows[:], 0.0).then_inc(s_pad, 1)
            eng.memset(k_rows[:], 0.0).then_inc(s_pad, 1)
            eng.memset(diag[:], 0.0).then_inc(s_pad, 1)
            eng.memset(v_rows[:], 0.0).then_inc(s_pad, 1)
            eng.wait_ge(s_pad, 4)
            eng.memset(v_rows[:, :, :, D:D + 1], 1.0).then_inc(s_pad, 1)
            eng.affine_select(out=diag[:], in_=diag[:], compare_op=ALU.is_ge, fill=-1.0e30,
                              base=0, pattern=[[-1, P]], channel_multiplier=1).then_inc(s_pad, 1)
            eng.memset(zeros[:], 0.0).then_inc(s_pad, 1)
            eng.memset(wo[:], 0.0).then_inc(s_pad, 1)
            eng.memset(pick[:], 0.0).then_inc(s_pad, 1)
            eng.wait_ge(s_pad, 9)
            eng.affine_select(out=pick[:], in_=pick[:], compare_op=ALU.not_equal, fill=1.0,
                              base=-D, pattern=[[-HV, HG], [0, HV]], channel_multiplier=1).then_inc(s_pad, 1)
            for r, job in enumerate(ROTARY_JOBS):
                eng.wait_ge(s_rm, 2 * (r + 1))
                eng.wait_ge(s_vr, job)
                rows, done = (k_rows, s_kr) if r < TT else (q_rows, s_qr)
                eng.tensor_tensor(rows[:, r % TT, :, 0:RD], rot[r % 2][:, 0, :, :], rot[r % 2][:, 1, :, :], ALU.add).then_inc(done, 1)

        @block.vector
        def _(dve):
            st = Steps(dve, s_st)
            v = nc.vector
            job = [0]

            def vjob():
                job[0] += 1
                dve.wait_ge(s_vw, job[0])
                return vbank[(job[0] - 1) % 4]

            dve.wait_ge(t["s_ln"], 2 * TT)
            v.tensor_scalar(sd[:, :, 0], mv[:, :, 1], LN_EPS, None, ALU.add).then_inc(s_var, 1)
            dve.wait_ge(s_sd, 1)
            st.link(v.reciprocal(sd[:, :, 0], sd[:, :, 1]))
            for i in range(TT):
                v.tensor_scalar(xn[:, i, :], x1[:, i, :], mv[:, i, 0:1], sd[:, i, 0:1],
                                ALU.subtract, ALU.mult).then_inc(s_xn, 1)
            for k in range(KT):
                v.tensor_copy(xT[:, k, :], vjob()).then_inc(s_vr, 1)

            bank = vjob()
            v.tensor_copy(kv[:].rearrange("p a c -> p (a c)"), bank[:, 0:TT * RK]).then_inc(s_vr, 1)
            dve.wait_ge(s_vr, job[0])
            st.link(v.tensor_tensor(kv2[:], kv[:], kv[:], ALU.mult))
            st.link(v.reduce_sum(ms[:], kv2[:], AXX))
            v.tensor_scalar(rms[:], ms[:], 1.0 / RK, 1e-6, ALU.mult, ALU.add).then_inc(s_ms, 1)

            def rotate(r):
                i = r % TT
                bank = vjob().rearrange("p (h d) -> p h d", d=RD)
                assert job[0] == ROTARY_JOBS[r]
                cos = w["cos"][:, i % 2, :].unsqueeze(1)
                sin = w["sin"][:, i % 2, :].unsqueeze(1)
                h2 = RD // 2
                if r >= 2:
                    dve.wait_ge(s_kr, min(r - 1, TT))
                    if r - 1 > TT:
                        dve.wait_ge(s_qr, r - 1 - TT)
                v.tensor_tensor(rot[r % 2][:, 0, :, :], bank, cos.to_broadcast([P, H, RD]), ALU.mult).then_inc(s_rm, 1)
                v.tensor_tensor(rot[r % 2][:, 1, :, 0:h2], bank[:, :, h2:RD], sin[:, :, 0:h2].to_broadcast([P, H, h2]), ALU.mult).then_inc(s_rm, 1)
                v.tensor_tensor(rot[r % 2][:, 1, :, h2:RD], bank[:, :, 0:h2], sin[:, :, h2:RD].to_broadcast([P, H, h2]), ALU.mult).then_inc(s_vr, 1)

            rotate(0)
            rotate(1)
            dve.wait_ge(s_rms, 1)
            st.link(v.reciprocal(ms[:], rms[:]))
            v.tensor_tensor(kv2[:], kv[:], ms[:].unsqueeze(2).to_broadcast([P, TT, RK]), ALU.mult).then_inc(s_kvn, 1)
            rotate(2)
            bank = vjob()
            v.tensor_scalar(kvT[:], bank[0:RK, :], w["g"][:, 0:1], None, ALU.mult).then_inc(s_vr, 1)
            for r in range(3, 2 * TT):
                rotate(r)

            def maxima(u):
                b, q, g = units[u]
                n = P * (q + 1)
                dve.wait_ge(s_s, u + 1)
                if u >= 2:
                    dve.wait_ge(s_p, u - 1)
                rows = pairs[u % 2][:].rearrange("p a (c n) -> p c a n", c=2)
                st.link(v.reduce_max(top[:, u % 2, :].rearrange("p (c a) -> p c a", a=2), rows[:, :, :, 0:n], AXX))
                v.tensor_scalar(ntop[:, u % 2, :], top[:, u % 2, :], -SCALE, None, ALU.mult).then_inc(s_nt, 1)

            def copy_output(m):
                b, q, g = units[2 * m]
                dve.wait_ge(s_o, 2 * m + 2)
                v.tensor_copy(oT[:, g, b * T:(b + 1) * T], pairs[3][:, m % 2, 0:T]).then_inc(s_oc, 1)

            def norm_output(m, parts=1):
                b, q, g = units[2 * m]
                dve.wait_ge(s_ps, m + 1)
                n = T // parts
                for part in range(parts):
                    own = slice(part * n, (part + 1) * n)
                    st.link(v.reciprocal(rtot[:, own], pairs[3][:, m % 2, T + part * n:T + (part + 1) * n]))
                    rows = oT[:, g, b * T + part * n:b * T + (part + 1) * n]
                    v.tensor_tensor(rows, rows, rtot[:, own], ALU.mult).then_inc(s_on, 1)

            maxima(0)
            maxima(1)
            for u in range(NU):
                if u + 2 < NU:
                    maxima(u + 2)
                if u >= 2 and u % 2 == 0:
                    copy_output(u // 2 - 1)
                if u >= 2 and u % 2 == 1:
                    norm_output(u // 2 - 1)
            copy_output(NU // 2 - 1)
            for i in range(TT):
                if i == 1:
                    norm_output(NU // 2 - 1, 2)
                dve.wait_ge(s_y, i + 1)
                add_rows(v, dve, t, i, pairs[i // 2][:, i % 2, 0:C], t["s_x2"], 2 * TT)

        @block.scalar
        def _(act):
            job = [0]

            def ajob():
                job[0] += 1
                act.wait_ge(s_aw, job[0])
                return abank[(job[0] - 1) % 4]

            act.wait_ge(s_var, 1)
            act.activation(sd[:, :, 1], sd[:, :, 0], ACT.Sqrt).then_inc(s_sd, 1)
            act.activation(qcT[:], ajob(), ACT.Copy).then_inc(s_ar, 1)
            act.wait_ge(s_ms, 1)
            act.activation(rms[:], rms[:], ACT.Sqrt).then_inc(s_rms, 1)
            act.wait_ge(s_pad, 4)

            def content(i):
                bank = ajob()
                act.activation(q_rows[:, i, :, RD:HD], bank[:, 0:C].rearrange("p (h d) -> p h d", d=D), ACT.Copy).then_inc(s_qr2, 1)
                act.activation(k_rows[:, i, :, RD:HD], bank[:, C:2 * C].rearrange("p (h d) -> p h d", d=D), ACT.Copy).then_inc(s_ar, 1)
                act.activation(v_rows[:, i, :, 0:D], ajob()[:, 0:C].rearrange("p (h d) -> p h d", d=D), ACT.Copy).then_inc(s_ar, 1)

            def copy_rows(i):
                for h in range(2):
                    for rows in (qT, kT):
                        act.activation(rows[:, 4 * h:4 * h + 4, i * P:(i + 1) * P],
                                       ajob().rearrange("p (a n) -> p a n", a=4), ACT.Copy).then_inc(s_ar, 1)

            for i in range(TT):
                content(i)
                if i >= 2:
                    copy_rows(i - 2)
            copy_rows(TT - 2)
            copy_rows(TT - 1)

            def probabilities(u):
                b, q, g = units[u]
                n = P * (q + 1)
                act.wait_ge(s_nt, u + 1)
                if u >= 2:
                    act.wait_ge(s_t, u - 1)
                for j in range(HG):
                    c = (j // 2) * T
                    ins = act.activation(pr[u % 2][:, j, 0:n], pairs[u % 2][:, j % 2, c:c + n], ACT.Exp, bias=ntop[:, u % 2, j:j + 1],
                                         scale=SCALE)
                ins.then_inc(s_p, 1)

            def copy_probs(u):
                b, q, g = units[u]
                act.wait_ge(s_t, u + 1)
                if u >= 2:
                    act.wait_ge(s_o, u - 1)
                act.activation(prT[u % 2][:, :, 0:q + 1, :],
                               pairs[2][:].rearrange("p a c -> p (a c)").rearrange("p (j k n) -> p j k n", j=HG, k=2)[:, :, 0:q + 1, :],
                               ACT.Copy).then_inc(s_tc, 1)

            probabilities(0)
            for u in range(NU):
                if u + 1 < NU:
                    probabilities(u + 1)
                copy_probs(u)
            act.activation(sd[:, :, 1], sd[:, :, 1], ACT.Sqrt)

        @block.tensor
        def _(pe):
            nv, na = [0], [0]

            def vring():
                nv[0] += 1
                if nv[0] > 4:
                    pe.wait_ge(s_vr, nv[0] - 4)
                return vbank[(nv[0] - 1) % 4]

            def aring():
                na[0] += 1
                if na[0] > 4:
                    pe.wait_ge(s_ar, na[0] - 4)
                return abank[(na[0] - 1) % 4]

            pe.wait_ge(s_xn, TT)
            for k in range(KT):
                bank = vring()
                for i in range(TT):
                    mm = pe.transpose(bank[:, i * P:(i + 1) * P], xn[:, i, k * P:(k + 1) * P], ident[:, :])
                mm.then_inc(s_vw, 1)
            pe.wait_ge(s_vr, KT)
            bank = aring()
            for k in range(KT):
                mm = pe.matmul(bank, w["wq"][:, k, :], xT[:, k, :], start=(k == 0), stop=(k == KT - 1))
            mm.then_inc(s_aw, 1)
            bank = vring()
            for i in range(TT):
                for k in range(KT):
                    mm = pe.matmul(bank[:, i * RK:(i + 1) * RK], xT[:, k, i * P:(i + 1) * P], w["wkv"][:, k, :],
                                   start=(k == 0), stop=(k == KT - 1))
            mm.then_inc(s_vw, 1)
            def rotary_keys(i):
                bank = vring()
                for k in range(KT):
                    mm = pe.matmul(bank, xT[:, k, i * P:(i + 1) * P], w["wkr"][:, k, :], start=(k == 0), stop=(k == KT - 1))
                mm.then_inc(s_vw, 1)

            for i in range(3):
                rotary_keys(i)
            pe.wait_ge(s_kvn, 1)
            bank = vring()
            for i in range(TT):
                mm = pe.transpose(bank[0:RK, i * P:(i + 1) * P], kv2[:, i, :], ident[:, :])
            mm.then_inc(s_vw, 1)
            latent = nv[0]
            rotary_keys(3)
            pe.wait_ge(s_ar, 1)
            pe.wait_ge(s_vr, latent)
            content = []

            def tile_products(i):
                bank = aring()
                pe.matmul(bank[:, 0:C], qcT[:, i * P:(i + 1) * P], w["wqd"][:, :], start=True, stop=True)
                pe.matmul(bank[:, C:2 * C], kvT[:, i * P:(i + 1) * P], w["wkd"][:, :], start=True, stop=True).then_inc(s_aw, 1)
                content.append(na[0])
                pe.matmul(aring()[:, 0:C], kvT[:, i * P:(i + 1) * P], w["wvd"][:, :], start=True, stop=True).then_inc(s_aw, 1)
                pe.matmul(vring(), qcT[:, i * P:(i + 1) * P], w["wqr"][:, :], start=True, stop=True).then_inc(s_vw, 1)

            def tile_transposes(i):
                pe.wait_ge(s_qr, i + 1)
                pe.wait_ge(s_kr, i + 1)
                pe.wait_ge(s_qr2, i + 1)
                pe.wait_ge(s_ar, content[i])
                for h in range(2):
                    for rows in (q_rows, k_rows):
                        bank = aring()
                        for a in range(4):
                            c = 2 * (4 * h + a)
                            mm = pe.transpose(bank[:, a * P:(a + 1) * P],
                                              rows[:, i, c:c + 2, :].rearrange("p h d -> p (h d)"), ident[:, :])
                        mm.then_inc(s_aw, 1)

            for i in range(TT):
                tile_products(i)
                if i >= 2:
                    tile_transposes(i - 2)
            tile_transposes(TT - 2)
            tile_transposes(TT - 1)
            pe.wait_ge(s_vr, nv[0])
            pe.wait_ge(s_ar, na[0])
            pe.wait_ge(s_pad, 10)

            def unit_scores(u):
                b, q, g = units[u]
                n = P * (q + 1)
                i = 2 * b + q
                if u >= 2:
                    pe.wait_ge(s_p, u - 1)
                for j in range(HG):
                    h = g * HG + j
                    r = HS * (h % 2)
                    pe.matmul(pairs[u % 2][:, j % 2, (j // 2) * T:(j // 2) * T + n],
                              qT[r:r + HD, h // 2, i * P:(i + 1) * P], kT[r:r + HD, h // 2, b * T:b * T + n],
                              start=True, stop=False)
                    c = (j // 2) * T + q * P
                    mm = pe.matmul(pairs[u % 2][:, j % 2, c:c + P], identb[:, :], diag[:], start=False, stop=True)
                mm.then_inc(s_s, 1)

            def unit_transposes(u):
                b, q, g = units[u]
                pe.wait_ge(s_p, u + 1)
                if u >= 1:
                    pe.wait_ge(s_tc, u)
                for j in range(HG):
                    for k in range(q + 1):
                        c = (2 * j + k) * P
                        mm = pe.transpose(pairs[2][:].rearrange("p a c -> p (a c)")[:, c:c + P],
                                          pr[u % 2][:, j, k * P:(k + 1) * P], ident[:, :])
                mm.then_inc(s_t, 1)

            def unit_values(u):
                b, q, g = units[u]
                pe.wait_ge(s_tc, u + 1)
                m = u // 2
                if m >= 2:
                    pe.wait_ge(s_on, m - 1)
                for k in range(q + 1):
                    for j in range(HG):
                        mm = pe.matmul(pairs[3][j * HV:(j + 1) * HV, m % 2, q * P:(q + 1) * P], v_rows[:, 2 * b + k, g * HG + j, :],
                                       prT[u % 2][:, j, k, :], start=(k == 0), stop=(k == q))
                mm.then_inc(s_o, 1)

            def spread_sums(m):
                b, q, g = units[2 * m]
                pe.wait_ge(s_oc, m + 1)
                pe.matmul(pairs[3][:, m % 2, T:2 * T], pick[:].rearrange("p j e -> p (j e)"), oT[:, g, b * T:(b + 1) * T],
                          start=True, stop=True).then_inc(s_ps, 1)

            def project_rows(i):
                b, q = i // 2, i % 2
                pe.wait_ge(s_on, (b + 1) * (NU // 2 // B) + (q if b == B - 1 else 0))
                pe.wait_ge(s_wo, HG * 16)
                for g in range(H // HG):
                    mm = pe.matmul(pairs[b][:, q, 0:C], oT[:, g, i * P:(i + 1) * P], wo[:, g, :],
                                   start=(g == 0), stop=(g == H // HG - 1))
                mm.then_inc(s_y, 1)

            unit_scores(0)
            unit_scores(1)
            unit_transposes(0)
            for u in range(NU):
                if u + 2 < NU:
                    unit_scores(u + 2)
                if u + 1 < NU:
                    unit_transposes(u + 1)
                if u >= 2 and u % 2 == 1:
                    spread_sums(u // 2 - 1)
                unit_values(u)
                if u == NU - 2:
                    project_rows(0)
            spread_sums(NU // 2 - 1)
            for i in range(1, TT):
                project_rows(i)


def expert_layer(nc, t, out):
    with ExitStack() as ctx:
        def sb(name, shape, dt=F32):
            return ctx.enter_context(nc.sbuf_tensor(name, shape, dt))

        def ps(name, shape):
            return ctx.enter_context(nc.psum_tensor(name, shape, F32))

        def sem(name):
            return ctx.enter_context(nc.semaphore(name))

        x2, ident, w2, b1, b2, rw, rb, cst = (t[n] for n in ("x1", "ident", "w2", "b1", "b2", "rw", "rb", "cst"))
        slots, y_slots = t["slots"], nc.dram_tensor("y_slots", [TILES * P, C], F32).ap()
        mv = t["mv"]
        sd = sb("f_sd", [P, TT, 2])
        xn = sb("f_xn", [P, TT, C])
        xT = sb("f_xT", [P, KT, TOK])
        logit = sb("logit", [P, TT, E])
        less = sb("less", [P, TT, E])
        ex = sb("ex", [P, TT, E])
        best = sb("best", [P, TT])
        esum = sb("esum", [P, TT])
        gate = sb("gate", [P, TT])
        tie = sb("tie", [P, TT, E])
        first = sb("first", [P, TT])
        chosen = sb("chosen", [P, TT, E])
        chosenb = sb("chosenb", [P, TT, E], BF16)
        upper = sb("upper", [P, P], BF16)
        onesb = sb("onesb", [P, P], BF16)
        over = sb("over", [P, E, TT])
        tiles = sb("tiles", [P, E])
        before = sb("before", [P, E, E])
        start = sb("start", [P, E])
        end = sb("end", [P, E])
        place = sb("place", [P, TT, E])
        slot = sb("slot", [P, TT])
        slot_u = sb("slot_u", [P, TT], mybir.dt.uint32)
        done = sb("done", [P, TILES, E])
        expert = sb("expert", [P, TILES])
        expert_i = sb("expert_i", [P, TILES], mybir.dt.int32)
        xs = sb("xs", [P, TILES, C])
        xsT = sb("xsT", [P, TILES, KT, P])
        w1 = [sb(f"w1_{i}", [P, KT, F]) for i in range(2)]
        hT = [sb(f"hT{i}", [P, FT, P]) for i in range(2)]
        ys = [sb(f"ys{i}", [P, C]) for i in range(2)]
        yg = sb("yg", [P, TT, C])
        bank = [ps(f"f_bank{i}", [P, 512]) for i in range(2)]
        hp = [ps(f"h_bank{i}", [P, FT, P]) for i in range(2)]
        yp = [ps(f"y_bank{i}", [P, C]) for i in range(2)]

        s_st = sem("f_steps")
        s_var = sem("f_variance_ready")
        s_sd = sem("f_deviation_ready")
        s_xn = sem("f_normed_ready")
        s_xt = sem("f_transposed")
        s_xts = sem("f_transposed_copied")
        s_lg = sem("logits_ready")
        s_ls = sem("logits_shifted")
        s_ex = sem("logits_exp_ready")
        s_c = sem("choice_ready")
        s_tri = sem("triangle_ready")
        s_rk = sem("ranks_ready")
        s_slot = sem("slots_ready")
        s_te = sem("tile_experts_ready")
        s_sc = sem("rows_scattered")
        s_xs = [sem(f"slot_rows_in_{i}") for i in range(2)]
        s_st_t = sem("slot_rows_transposed")
        s_st_c = sem("slot_rows_copied")
        s_w1 = [sem(f"w1_in_{i}") for i in range(2)]
        s_h = sem("hidden_product")
        s_hr = sem("hidden_ready")
        s_y = sem("tile_product")
        s_ys = sem("tile_rows_ready")
        s_yo = [sem(f"tile_rows_stored_{i}") for i in range(2)]
        s_yg = [sem(f"rows_gathered_{i}") for i in range(TT)]
        s_f = sem("final_rows_ready")
        s_out = sem("out_stored")
        block = ctx.enter_context(nc.Block())

        FIRST_TILES = 2

        def expert_of(eng, tile):
            return eng.value_load(expert_i[0:1, bass.ds(tile, 1)], min_val=0, max_val=E - 1)

        @block.gpsimd
        def _(eng):
            eng.memset(onesb[:], 1.0).then_inc(s_tri, 1)
            eng.wait_ge(s_tri, 1)
            eng.affine_select(out=upper[:], in_=onesb[:], compare_op=ALU.is_gt, fill=0.0,
                              base=0, pattern=[[1, P]], channel_multiplier=-1).then_inc(s_tri, 1)
            eng.wait_ge(s_slot, 1)
            eng.wait_ge(t["s_zero"], 16)
            for i in range(TT):
                eng.indirect_dma_start(slots, bass.IndirectOffsetOnAxis(ap=slot_u[:, i:i + 1], axis=0), xn[:, i, :], None).then_inc(s_sc, 16)
            for i in range(2):
                eng.wait_ge(s_yo[i], 16 * ((TILES + 1 - i) // 2))
            for i in range(TT):
                eng.indirect_dma_start(yg[:, i, :], None, y_slots, bass.IndirectOffsetOnAxis(ap=slot_u[:, i:i + 1], axis=0)).then_inc(s_yg[i], 16)

        @block.sync
        def _(sp):
            def load_w1(s, tile):
                e = expert_of(sp, tile)
                sp.dma_start(w1[s][:], t["w1_in"][bass.ds(e, 1), :, :].rearrange("o (k p) n -> p (o k) n", p=P)).then_inc(s_w1[s], 16)

            def store(s, tile):
                sp.wait_ge(s_ys, tile + 1)
                sp.dma_start(y_slots[bass.ds(tile * P, P), :], ys[s][:]).then_inc(s_yo[s], 16)

            sp.wait_ge(s_te, 1)
            load_w1(0, 0)
            sp.wait_ge(s_sc, 16 * TT)
            slot_rows = slots.rearrange("(t p) c -> p t c", p=P)
            sp.dma_start(xs[:, 0:FIRST_TILES, :], slot_rows[:, 0:FIRST_TILES, :]).then_inc(s_xs[0], 16)
            load_w1(1, 1)
            sp.dma_start(xs[:, FIRST_TILES:TILES, :], slot_rows[:, FIRST_TILES:TILES, :]).then_inc(s_xs[1], 16)
            with sp.Fori(0, (TILES - 3) // 2) as it:
                for s in range(2):
                    tile = it * 2 + s
                    sp.wait_ge(s_h, tile + 1)
                    load_w1(s, tile + 2)
                    store(s, tile)
            sp.wait_ge(s_h, TILES - 2)
            load_w1(0, TILES - 1)
            for n in range(TILES - 3, TILES):
                store(n % 2, n)
            rows = out.rearrange("b (q p) c -> p (b q) c", p=P)
            for i in range(TT):
                sp.wait_ge(s_f, i + 1)
                sp.dma_start(rows[:, i, :], x2[:, i, :]).then_inc(s_out, 16)
            sp.wait_ge(s_out, 16 * TT)

        @block.vector
        def _(dve):
            st = Steps(dve, s_st)
            v = nc.vector
            dve.wait_ge(t["s_ln"], 4 * TT)
            v.tensor_scalar(sd[:, :, 0], mv[:, :, 1], LN_EPS, None, ALU.add).then_inc(s_var, 1)
            dve.wait_ge(s_sd, 1)
            st.link(v.reciprocal(sd[:, :, 0], sd[:, :, 1]))
            for i in range(TT):
                v.tensor_scalar(xn[:, i, :], x2[:, i, :], mv[:, i, 0:1], sd[:, i, 0:1],
                                ALU.subtract, ALU.mult).then_inc(s_xn, 1)
            dve.wait_ge(s_xt, 1)
            v.tensor_copy(xT[:, 0, :], bank[0][:, :]).then_inc(s_xts, 1)

            dve.wait_ge(t["s_fw"], 16 * t["n_fw"])
            dve.wait_ge(s_lg, 1)
            st.link(v.tensor_tensor(logit[:], bank[0][:, 0:TT * E].rearrange("p (i e) -> p i e", e=E),
                                    rb[:].unsqueeze(1).to_broadcast([P, TT, E]), ALU.add))
            st.link(v.reduce_max(best[:], logit[:], AXX))
            high = best[:].unsqueeze(2).to_broadcast([P, TT, E])
            v.tensor_tensor(less[:], logit[:], high, ALU.subtract).then_inc(s_ls, 1)
            st.link(v.tensor_tensor(tie[:], logit[:], high, ALU.is_ge))
            st.link(v.tensor_tensor(tie[:], tie[:], cst["fall"].unsqueeze(1).to_broadcast([P, TT, E]), ALU.mult))
            st.link(v.reduce_max(first[:], tie[:], AXX))
            st.link(v.tensor_tensor(chosen[:], tie[:], first[:].unsqueeze(2).to_broadcast([P, TT, E]), ALU.is_equal))
            v.tensor_copy(chosenb[:], chosen[:]).then_inc(s_c, 1)
            dve.wait_ge(s_ex, 1)
            st.link(v.reduce_sum(esum[:], ex[:], AXX))
            st.link(v.reciprocal(gate[:], esum[:]))

            dve.wait_ge(s_rk, 1)
            ranks = bank[1][:, 0:TT * E].rearrange("p (i e) -> p i e", e=E)
            counts = bank[1][:, TT * E:(TT + 1) * E]
            st.link(v.tensor_tensor(over[:], counts.unsqueeze(2).to_broadcast([P, E, TT]),
                                    cst["fill"].unsqueeze(1).to_broadcast([P, E, TT]), ALU.is_gt))
            st.link(v.reduce_sum(tiles[:], over[:], AXX))
            st.link(v.tensor_tensor(before[:], tiles[:].unsqueeze(1).to_broadcast([P, E, E]),
                                    cst["lower"].rearrange("p (a b) -> p a b", b=E), ALU.mult))
            st.link(v.reduce_sum(start[:], before[:], AXX))
            st.link(v.scalar_tensor_tensor(out=place[:], in0=start[:].unsqueeze(1).to_broadcast([P, TT, E]), scalar=float(P),
                                           in1=ranks, op0=ALU.mult, op1=ALU.add))
            st.link(v.tensor_tensor(place[:], place[:], chosen[:], ALU.mult))
            st.link(v.reduce_sum(slot[:], place[:], AXX))
            v.tensor_copy(slot_u[:], slot[:]).then_inc(s_slot, 1)
            st.link(v.tensor_tensor(end[:], start[:], tiles[:], ALU.add))
            st.link(v.tensor_tensor(done[:], end[:].unsqueeze(1).to_broadcast([P, TILES, E]),
                                    cst["tile"].unsqueeze(2).to_broadcast([P, TILES, E]), ALU.is_le))
            st.link(v.reduce_sum(expert[:], done[:], AXX))
            v.tensor_scalar(expert_i[:], expert[:], float(E - 1), None, ALU.min).then_inc(s_te, 1)

            for n in range((TILES + 1) // 2):
                m = min(2, TILES - 2 * n)
                dve.wait_ge(s_st_t, n + 1)
                v.tensor_copy(xsT[:, 2 * n:2 * n + m, :, :].rearrange("p t k n -> p (t k n)"),
                              bank[n % 2][:, 0:m * C]).then_inc(s_st_c, 1)

            def tile_rows(s, tile, used):
                e = expert_of(dve, tile)
                dve.wait_ge(s_y, tile + 1)
                wait_past(dve, s_yo[s], 16 * used)
                v.tensor_tensor(ys[s][:].unsqueeze(1), yp[s][:].unsqueeze(1), b2[:, bass.ds(e, 1), :], ALU.add).then_inc(s_ys, 1)

            dve.wait_ge(s_te, 1)
            for s in range(2):
                tile_rows(s, s, 0)
            with dve.Fori(1, (TILES - 1) // 2) as it:
                for s in range(2):
                    tile_rows(s, it * 2 + s, it)
            tile_rows(0, TILES - 1, (TILES - 1) // 2)

            for i in range(TT):
                dve.wait_ge(s_yg[i], 16)
                v.scalar_tensor_tensor(out=x2[:, i, :], in0=yg[:, i, :], scalar=gate[:, i:i + 1], in1=x2[:, i, :],
                                       op0=ALU.mult, op1=ALU.add).then_inc(s_f, 1)

        @block.scalar
        def _(act):
            act.wait_ge(s_var, 1)
            act.activation(sd[:, :, 1], sd[:, :, 0], ACT.Sqrt).then_inc(s_sd, 1)
            act.wait_ge(s_xt, 2)
            act.activation(xT[:, 1, :], bank[1][:, :], ACT.Copy).then_inc(s_xts, 1)
            act.wait_ge(s_ls, 1)
            act.activation(ex[:], less[:], ACT.Exp).then_inc(s_ex, 1)

            def hidden(s, tile):
                e = expert_of(act, tile)
                act.wait_ge(s_h, tile + 1)
                for f in range(FT):
                    act.activation(hT[s][:, f, :], hp[s][:, f, :], ACT.Relu,
                                   bias=b1[:, bass.ds(e * FT + f, 1)]).then_inc(s_hr, 1)

            act.wait_ge(s_te, 1)
            with act.Fori(0, (TILES - 1) // 2) as it:
                for s in range(2):
                    hidden(s, it * 2 + s)
            hidden(0, TILES - 1)

        @block.tensor
        def _(pe):
            for i in range(TT):
                pe.wait_ge(s_xn, i + 1)
                for k in range(KT):
                    mm = pe.transpose(bank[k][:, i * P:(i + 1) * P], xn[:, i, k * P:(k + 1) * P], ident[:, :])
                    if i == TT - 1:
                        mm.then_inc(s_xt, 1)
            pe.wait_ge(s_xts, KT)
            for i in range(TT):
                for k in range(KT):
                    mm = pe.matmul(bank[0][:, i * E:(i + 1) * E], xT[:, k, i * P:(i + 1) * P], rw[:, k, :],
                                   start=(k == 0), stop=(k == KT - 1))
            mm.then_inc(s_lg, 1)
            pe.wait_ge(s_tri, 2)
            pe.wait_ge(s_c, 1)
            for i in range(TT + 1):
                for j in range(min(i, TT)):
                    mm = pe.matmul(bank[1][:, i * E:(i + 1) * E], onesb[:, :], chosenb[:, j, :],
                                   start=(j == 0), stop=(i == TT and j == TT - 1))
                if i < TT:
                    mm = pe.matmul(bank[1][:, i * E:(i + 1) * E], upper[:, :], chosenb[:, i, :], start=(i == 0), stop=True)
            mm.then_inc(s_rk, 1)
            def transpose_rows(pairs):
                for n in pairs:
                    if n >= 2:
                        pe.wait_ge(s_st_c, n - 1)
                    for i in range(min(2, TILES - 2 * n)):
                        for k in range(KT):
                            mm = pe.transpose(bank[n % 2][:, (i * KT + k) * P:(i * KT + k + 1) * P],
                                              xs[:, 2 * n + i, k * P:(k + 1) * P], ident[:, :])
                    mm.then_inc(s_st_t, 1)

            pe.wait_ge(s_xs[0], 16)
            pe.wait_ge(s_te, 1)
            transpose_rows(range(FIRST_TILES // 2))
            pe.wait_ge(s_st_c, FIRST_TILES // 2)

            def hidden(s, tile, uses):
                pe.wait_ge(s_w1[s], 16 * (uses + 1))
                wait_past(pe, s_hr, (tile - 1) * FT)
                for f in range(FT):
                    for k in range(KT):
                        mm = pe.matmul(hp[s][:, f, :], w1[s][:, k, f * P:(f + 1) * P],
                                       xsT[:, bass.ds(tile, 1), k, :].rearrange("p o n -> p (o n)"),
                                       start=(k == 0), stop=(k == KT - 1))
                mm.then_inc(s_h, 1)

            def rows(s, tile):
                e = expert_of(pe, tile)
                if not isinstance(tile, int) or tile >= 2:
                    pe.wait_ge(s_ys, tile - 1)
                for f in range(FT):
                    pe.wait_ge(s_hr, tile * FT + (f + 1))
                    mm = pe.matmul(yp[s][:], hT[s][:, f, :], w2[:, bass.ds(e * FT + f, 1), :].rearrange("p o c -> p (o c)"),
                                   start=(f == 0), stop=(f == FT - 1))
                mm.then_inc(s_y, 1)

            pe.wait_ge(t["s_fw"], 16 * t["n_fw"])
            hidden(0, 0, 0)
            pe.wait_ge(s_xs[1], 16)
            transpose_rows(range(FIRST_TILES // 2, (TILES + 1) // 2))
            hidden(1, 1, 0)
            pe.wait_ge(s_st_c, (TILES + 1) // 2)
            rows(0, 0)
            hidden(0, 2, 1)
            rows(1, 1)
            with pe.Fori(1, (TILES - 1) // 2) as it:
                hidden(1, it * 2 + 1, it)
                rows(0, it * 2)
                hidden(0, it * 2 + 2, it + 1)
                rows(1, it * 2 + 1)
            rows(0, TILES - 1)


def build(nc, a, out):
    with ExitStack() as ctx:
        def sb(name, shape, dt=F32):
            return ctx.enter_context(nc.sbuf_tensor(name, shape, dt))

        t = {"x1": sb("x1", [P, TT, C]), "ident": sb("ident", [P, P]), "identb": sb("identb", [P, P], BF16),
             "s_x1": ctx.enter_context(nc.semaphore("x1_ready")),
             "stats": sb("ln_stats", [P, TT, 6]), "mv": sb("ln_mv", [P, TT, 2]),
             "s_ln": ctx.enter_context(nc.semaphore("ln_statistics_ready")),
             "s_x2": ctx.enter_context(nc.semaphore("x2_ready")),
             "s_aw": ctx.enter_context(nc.semaphore("attention_weights_in")),
             "x_in": a["x"], "ctx": a["ctx_1024"]}
        for n in ("q", "k", "v", "o"):
            t["w" + n] = a["L0_xattn_W" + n]
            t["b" + n] = a["L0_xattn_b" + n]
        by_row = "(k p) n -> p k n"
        src = {"wq": a["L0_attn_W_q"].rearrange(by_row, p=P), "wkv": a["L0_attn_W_kv"].rearrange(by_row, p=P),
               "wkr": a["L0_attn_W_krope"].rearrange(by_row, p=P),
               "wqr": a["L0_attn_W_qrope"], "wqd": a["L0_attn_W_qdec"], "wkd": a["L0_attn_W_kdec"],
               "wvd": a["L0_attn_W_vdec"], "g": a["L0_attn_g_kv"].unsqueeze(1), "cos": a["cos"], "sin": a["sin"]}
        t["attn_w"] = {n: sb("a_" + n, s.shape) for n, s in src.items()}
        t["attn_src"] = src
        t["attn_wo"] = a["L0_attn_W_o"]
        cst = sb("cst", [P, sum(n for _, n in TABLES)])
        at = 0
        t["cst"] = {}
        for n, width in TABLES:
            t["cst"][n] = cst[:, at:at + width]
            at += width
        t["rw"], t["rb"] = sb("rw", [P, KT, E]), sb("rb", [P, E])
        t["b1"] = sb("b1", [P, E * FT])
        small = [(cst[:], a["tables"].partition_broadcast(P)), (t["rb"][:], a["L0_ffn_router_b"].partition_broadcast(P)),
                 (t["rw"][:], a["L0_ffn_router_W"].rearrange(by_row, p=P)), (t["b1"][:], a["L0_ffn_b1"])]
        t["ffn_small"] = small
        t["b2_in"], t["w2_in"], t["w1_in"] = a["L0_ffn_b2"], a["L0_ffn_W2"], a["L0_ffn_W1"]
        t["s_fw"] = ctx.enter_context(nc.semaphore("expert_weights_in"))
        t["s_zero"] = ctx.enter_context(nc.semaphore("slots_zeroed"))
        t["n_fw"] = len(small) + 2 * E
        t["slots"] = nc.dram_tensor("slots", [TILES * P, C], F32).ap()
        cross_attention(nc, t)
        t["b2"] = sb("b2", [P, E, C])
        t["w2"] = sb("w2", [P, E * FT, C])
        latent_attention(nc, t)
        expert_layer(nc, t, out)


TABLES = (("fall", E), ("fill", TT), ("lower", E * E), ("tile", TILES))


def routing_tables():
    return np.concatenate([np.arange(E, 0, -1), np.arange(TT) * P, np.tril(np.ones((E, E)), -1).ravel(),
                           np.arange(TILES)]).astype(np.float32)


def rope_tables():
    dim = 32
    inv_freq = 1.0 / 10000.0 ** (np.arange(0, dim, 2, dtype=np.float32) / dim)
    freqs = np.outer(np.arange(NQ, dtype=np.float32), inv_freq)
    cos, sin = np.cos(freqs), np.sin(freqs)
    lay = lambda a: np.ascontiguousarray(a.reshape(2, P, dim).transpose(1, 0, 2).astype(np.float32))
    return lay(np.concatenate([cos, cos], -1)), lay(np.concatenate([-sin, sin], -1))


_TRANSPOSED = ("L0_xattn_Wq", "L0_xattn_Wk", "L0_xattn_Wv", "L0_xattn_Wo")
_BY_CHANNEL = ("L0_xattn_bq", "L0_xattn_bk", "L0_xattn_bv")
_BY_GROUP = ("L0_xattn_Wq", "L0_xattn_bq", "L0_xattn_Wk", "L0_xattn_bk")
_INS = ["x", "ctx_1024", "L0_xattn_Wq", "L0_xattn_bq", "L0_xattn_Wk", "L0_xattn_bk", "L0_xattn_Wv", "L0_xattn_bv",
        "L0_xattn_Wo", "L0_xattn_bo", "L0_attn_W_kv", "L0_attn_g_kv", "L0_attn_W_kdec", "L0_attn_W_vdec",
        "L0_attn_W_q", "L0_attn_W_qdec", "L0_attn_W_krope", "L0_attn_W_qrope", "L0_attn_W_o",
        "L0_ffn_router_W", "L0_ffn_router_b", "L0_ffn_W1", "L0_ffn_b1", "L0_ffn_W2", "L0_ffn_b2"]


def kernel(**inputs):
    import concourse.bacc as bacc
    from concourse.bass_utils import run_bass_kernel_spmd as run

    nc = bacc.Bacc("TRN2", target_bir_lowering=False, num_devices=1)
    arrays, aps = {}, {}
    for name in _INS:
        arr = np.asarray(inputs[name])
        if name == "L0_ffn_b1":
            arr = np.ascontiguousarray(arr.reshape(-1, P).T)
        if name in _BY_GROUP:
            arr = arr.reshape(2, GROUPS // 2, HG, D, -1).transpose(1, 0, 3, 2, 4).reshape(arr.shape)
        if name in _BY_CHANNEL:
            arr = arr.reshape(-1, P)
        arr = np.ascontiguousarray(arr.T if name in _TRANSPOSED + _BY_CHANNEL else arr)
        arrays["in_" + name] = arr
        aps[name] = nc.dram_tensor("in_" + name, arr.shape, mybir.dt.from_np(arr.dtype), kind="ExternalInput").ap()
    for name, arr in zip(("cos", "sin", "tables"), (*rope_tables(), routing_tables())):
        arrays["in_" + name] = arr
        aps[name] = nc.dram_tensor("in_" + name, arr.shape, F32, kind="ExternalInput").ap()
    out = nc.dram_tensor("out_0", (B, NQ, C), F32, kind="ExternalOutput").ap()
    build(nc, aps, out)
    r = run(nc, [arrays], core_ids=[0])
    return r.results[0]["out_0"]
```
